# Optimizing a Trainium2 kernel written in Bass

```python
import numpy as np
import jax
import jax.numpy as jnp

def _softmax(x, axis=-1):
    return jax.nn.softmax(x, axis=axis)

def _gelu(x):
    return jax.nn.gelu(x, approximate=True)

def _silu(x):
    return jax.nn.silu(x)

def _sigmoid(x):
    return jax.nn.sigmoid(x)

def _layernorm(x, axis=-1, eps=1e-05):
    m = jnp.mean(x, axis=axis, keepdims=True)
    v = jnp.var(x, axis=axis, keepdims=True)
    return (x - m) / jnp.sqrt(v + eps)

def _scatter_add(tgt, idx, src, axis=0):
    return tgt.at[idx].add(src)

def _segment_sum(src, seg, n):
    return jax.ops.segment_sum(src, seg, n)
kernel_name = 'mk_gnn_resnorm_d2_gnn_r8_6483c8'

def setup_inputs(seed: int=0):
    np.random.seed(seed)
    _w = jnp.asarray

    def _rec_inputs():
        import jax
        import jax.numpy as jnp
        _gk = jax.random.key(seed)
        x = -0.0003713 + 1 * jax.random.normal(jax.random.fold_in(_gk, 1), (6250, 256), jnp.float32)
        src = jax.random.randint(jax.random.fold_in(_gk, 2), (200000,), 0, 6250, jnp.int32)
        dst = jax.random.randint(jax.random.fold_in(_gk, 3), (200000,), 0, 6250, jnp.int32)
        _o = jnp.argsort(dst, stable=True)
        src = src[_o]
        dst = dst[_o]
        edge_attr_96 = -4.21973e-05 + 0.999841 * jax.random.normal(jax.random.fold_in(_gk, 13), (200000, 96), jnp.float32)
        edge_weight = jax.random.uniform(jax.random.fold_in(_gk, 15), (200000,), jnp.float32, 0.0, 1)
        return (x, src, dst, edge_attr_96, edge_weight)
    x, src, dst, edge_attr_96, edge_weight = _rec_inputs()

    def _L0_gnn_setup():
        import jax, jax.numpy as jnp
        import numpy as np
        N_NODES = 6250
        N_EDGES = 100000
        EDGE_F = 96
        NODE_F = 256
        GLOB_F = 64
        HIDDEN = 1024
        N_GRAPHS = 8
        MLP_IN = NODE_F + 3 * EDGE_F + GLOB_F
        key = jax.random.key(seed)
        ks = jax.random.split(key, 9)
        x = jax.random.normal(ks[0], (N_NODES, NODE_F), dtype=jnp.float32)
        edge_attr = jax.random.normal(ks[1], (N_EDGES, EDGE_F), dtype=jnp.float32)
        u = jax.random.normal(ks[2], (N_GRAPHS, GLOB_F), dtype=jnp.float32)
        W1 = jax.random.normal(ks[3], (MLP_IN, HIDDEN), dtype=jnp.float32) * (1.0 / np.sqrt(MLP_IN))
        b1 = jax.random.normal(ks[4], (HIDDEN,), dtype=jnp.float32) * 0.01
        W2 = jax.random.normal(ks[5], (HIDDEN, NODE_F), dtype=jnp.float32) * (1.0 / np.sqrt(HIDDEN))
        b2 = jax.random.normal(ks[6], (NODE_F,), dtype=jnp.float32) * 0.01
        edge_index = jax.random.randint(ks[7], (2, N_EDGES), 0, N_NODES, dtype=jnp.int64 if jax.config.jax_enable_x64 else jnp.int32)
        batch = jnp.sort(jax.random.randint(ks[8], (N_NODES,), 0, N_GRAPHS, dtype=jnp.int32))
        return {'x': x, 'edge_attr': edge_attr, 'u': u, 'W1': W1, 'b1': b1, 'W2': W2, 'b2': b2, 'edge_index': edge_index, 'batch': batch}
    _L0_gnn_all = _L0_gnn_setup()
    _L0_gnn_in = {k: v for k, v in _L0_gnn_all.items() if k in ('u', 'W1', 'b1', 'W2', 'b2')}
    del _L0_gnn_all

    def _L1_gnn_setup():
        import jax, jax.numpy as jnp
        import numpy as np
        N = 6250
        E = 100000
        D_IN, D_HID, D_OUT = (256, 512, 256)
        LN_EPS = 1e-05

        def _layer_norm(x, g, b):
            mu = jnp.mean(x, axis=-1, keepdims=True)
            var = jnp.mean(jnp.square(x - mu), axis=-1, keepdims=True)
            return (x - mu) * jax.lax.rsqrt(var + LN_EPS) * g + b
        key = jax.random.key(seed)
        ks = jax.random.split(key, 8)
        return {'v': jax.random.normal(ks[0], (N, D_IN), dtype=jnp.float32), 'edge_weight': jax.random.uniform(ks[1], (E,), dtype=jnp.float32), 'epsilon': jnp.zeros((1, 1), dtype=jnp.float32), 'w1': jax.random.normal(ks[2], (D_HID, D_IN), dtype=jnp.float32) * (1.0 / np.sqrt(D_IN)), 'b1': jnp.zeros((D_HID,), dtype=jnp.float32), 'g1': jnp.ones((D_HID,), dtype=jnp.float32), 'beta1': jnp.zeros((D_HID,), dtype=jnp.float32), 'w2': jax.random.normal(ks[3], (D_OUT, D_HID), dtype=jnp.float32) * (1.0 / np.sqrt(D_HID)), 'b2': jnp.zeros((D_OUT,), dtype=jnp.float32), 'g2': jnp.ones((D_OUT,), dtype=jnp.float32), 'beta2': jnp.zeros((D_OUT,), dtype=jnp.float32), 'src': jax.random.randint(ks[4], (E,), 0, N, dtype=jnp.int32), 'dst': jax.random.randint(ks[5], (E,), 0, N, dtype=jnp.int32)}
    _L1_gnn_all = _L1_gnn_setup()
    _L1_gnn_in = {k: v for k, v in _L1_gnn_all.items() if k in ('epsilon', 'w1', 'b1', 'g1', 'beta1', 'w2', 'b2', 'g2', 'beta2')}
    del _L1_gnn_all
    return {'x': x, 'src': src, 'dst': dst, 'edge_attr_96': edge_attr_96, 'edge_weight': edge_weight, 'L0_gnn_u': _L0_gnn_in['u'], 'L0_gnn_W1': _L0_gnn_in['W1'], 'L0_gnn_b1': _L0_gnn_in['b1'], 'L0_gnn_W2': _L0_gnn_in['W2'], 'L0_gnn_b2': _L0_gnn_in['b2'], 'L1_gnn_epsilon': _L1_gnn_in['epsilon'], 'L1_gnn_w1': _L1_gnn_in['w1'], 'L1_gnn_b1': _L1_gnn_in['b1'], 'L1_gnn_g1': _L1_gnn_in['g1'], 'L1_gnn_beta1': _L1_gnn_in['beta1'], 'L1_gnn_w2': _L1_gnn_in['w2'], 'L1_gnn_b2': _L1_gnn_in['b2'], 'L1_gnn_g2': _L1_gnn_in['g2'], 'L1_gnn_beta2': _L1_gnn_in['beta2']}

def reference(x, src, dst, edge_attr_96, edge_weight, L0_gnn_u, L0_gnn_W1, L0_gnn_b1, L0_gnn_W2, L0_gnn_b2, L1_gnn_epsilon, L1_gnn_w1, L1_gnn_b1, L1_gnn_g1, L1_gnn_beta1, L1_gnn_w2, L1_gnn_b2, L1_gnn_g2, L1_gnn_beta2):
    import jax
    import jax.numpy as jnp

    def _L0_gnn_ref(x, edge_attr, u, W1, b1, W2, b2, edge_index, batch):
        import jax, jax.numpy as jnp
        import numpy as np
        N_NODES = 6250
        N_EDGES = 100000
        EDGE_F = 96
        NODE_F = 256
        GLOB_F = 64
        HIDDEN = 1024
        N_GRAPHS = 8
        MLP_IN = NODE_F + 3 * EDGE_F + GLOB_F
        col = edge_index[1]
        n = x.shape[0]
        out1 = jax.ops.segment_sum(edge_attr, col, num_segments=n)
        cnt = jax.ops.segment_sum(jnp.ones((edge_attr.shape[0], 1), edge_attr.dtype), col, num_segments=n)
        out2 = jax.ops.segment_max(edge_attr, col, num_segments=n)
        out2 = jnp.where(cnt > 0, out2, jnp.zeros_like(out2))
        out3 = out1 / jnp.maximum(cnt, 1.0)
        h = jnp.concatenate([x, out1, out2, out3, u[batch]], axis=1)
        h = jax.nn.relu(h @ W1 + b1) @ W2 + b2
        return h + x

    def _L1_gnn_ref(v, edge_weight, epsilon, w1, b1, g1, beta1, w2, b2, g2, beta2, src, dst):
        import jax, jax.numpy as jnp
        import numpy as np
        N = 6250
        E = 100000
        D_IN, D_HID, D_OUT = (256, 512, 256)
        LN_EPS = 1e-05

        def _layer_norm(x, g, b):
            mu = jnp.mean(x, axis=-1, keepdims=True)
            var = jnp.mean(jnp.square(x - mu), axis=-1, keepdims=True)
            return (x - mu) * jax.lax.rsqrt(var + LN_EPS) * g + b
        msgs = v[src] * edge_weight[:, None]
        agg = jax.ops.segment_sum(msgs, dst, num_segments=v.shape[0])
        h = agg + epsilon * v
        h = jax.nn.relu(_layer_norm(h @ w1.T + b1, g1, beta1))
        h = jax.nn.relu(_layer_norm(h @ w2.T + b2, g2, beta2))
        return h
    edge_index = jnp.stack([src, dst])
    batch0 = jnp.zeros((6250,), jnp.int32)
    x = _layernorm(x + _L0_gnn_ref(x, edge_attr_96, L0_gnn_u, L0_gnn_W1, L0_gnn_b1, L0_gnn_W2, L0_gnn_b2, edge_index, batch0), axis=-1)
    x = _layernorm(x + _L1_gnn_ref(x, edge_weight, L1_gnn_epsilon, L1_gnn_w1, L1_gnn_b1, L1_gnn_g1, L1_gnn_beta1, L1_gnn_w2, L1_gnn_b2, L1_gnn_g2, L1_gnn_beta2, src, dst), axis=-1)
    return x

_drawn_inputs = setup_inputs


def setup_inputs(seed=0):
    import zlib

    import numpy as np

    out = dict(_drawn_inputs(seed))
    spreads = {'L1_gnn_b1': (0.0, 0.8),
     'L1_gnn_g1': (1.0, 0.2),
     'L1_gnn_beta1': (0.0, 0.1),
     'L1_gnn_b2': (0.0, 0.1),
     'L1_gnn_g2': (1.0, 0.2),
     'L1_gnn_beta2': (0.0, 0.1)}
    factors = {'L0_gnn_b1': 8.0, 'L0_gnn_b2': 8.0}
    for name, (base, spread) in spreads.items():
        noise = np.random.default_rng([zlib.crc32(name.encode()), seed]).standard_normal(out[name].shape)
        drawn = base * np.exp(spread * noise) if base else spread * noise
        out[name] = jnp.asarray(drawn.astype(out[name].dtype))
    for name, factor in factors.items():
        out[name] = (out[name] * factor).astype(out[name].dtype)
    return out
```

```python
from contextlib import ExitStack

import numpy as np

import concourse.bass as bass
import concourse.mybir as mybir

ALU = mybir.AluOpType
ACT = mybir.ActivationFunctionType
AX = mybir.AxisListType
F32 = mybir.dt.float32
I32 = mybir.dt.int32

P = 128
N_NODES, N_EDGES = 6250, 200000
D, EF, GF, HID0, HID1 = 256, 96, 64, 1024, 512
BLOCKS = -(-N_NODES // P)
NP = BLOCKS * P
COLS = 4
GROUP = P * COLS
GROUPS = 8
STEP = GROUP * GROUPS
STEPS = BLOCKS
EP = STEPS * STEP
TILES = GROUPS * COLS
PAD_DEG = (EP - N_EDGES) // (NP - N_NODES)
WIN = 32
NPW = NP + WIN
CHUNK = 8
FULL = 7
SLOTS = (FULL + 1) * CHUNK
SPLIT = 448
ROWS_CHECK = 112
COLS_CHECK = EP // ROWS_CHECK
FINE_RING = 8
SKIP = float(1 << 20)
BIG = 3.4028234663852886e38
LN_EPS = 1e-5
KC = D // P
HC0 = HID0 // P
HC1 = HID1 // P
assert SPLIT * SPLIT == EP and EP - N_EDGES == PAD_DEG * (NP - N_NODES) and STEPS % 2 == 1


class Step:

    def __init__(self, i, par, uses):
        self.i, self.par, self.uses = i, par, uses

    def next(self):
        return Step(self.i + 1, 1 - self.par, self.uses + self.par)

    def before(self):
        return Step(self.i - 1, 1 - self.par, self.uses - (1 - self.par))

    def first(self):
        return isinstance(self.i, int) and self.i == 0

    def last(self):
        return isinstance(self.i, int) and self.i == STEPS - 1


def at(n):
    return Step(n, n % 2, n // 2)


def wait(eng, sem, value):
    if isinstance(value, int) and value <= 0:
        return
    eng.wait_ge(sem, value)


def pipelined(eng, step, last):
    step(at(0), None)
    step(at(1), at(0))
    with eng.Fori(1, STEPS // 2) as it:
        step(Step(it * 2, 0, it), Step(it * 2 - 1, 1, it - 1))
        step(Step(it * 2 + 1, 1, it), Step(it * 2, 0, it))
    step(at(STEPS - 1), at(STEPS - 2))
    last(at(STEPS - 1))


def over_blocks(eng, one):
    one(at(0))
    with eng.Fori(1, BLOCKS // 2 + 1) as it:
        one(Step(it * 2 - 1, 1, it - 1))
        one(Step(it * 2, 0, it))


def build(nc, t):
    ctx = ExitStack()

    def sb(name, shape, dt=F32):
        return ctx.enter_context(nc.sbuf_tensor(name, shape, dt))

    def bank(name):
        return ctx.enter_context(nc.psum_tensor(name, [P, 512], F32))

    def sem(name):
        return ctx.enter_context(nc.semaphore(name))

    with ctx:
        dst_rows_d = nc.dram_tensor("dst_rows_d", [SPLIT, SPLIT], F32).ap()
        x1_d = nc.dram_tensor("x1_d", [NP, D], F32).ap()

        w0x = sb("w0x", [P, KC, HID0])
        w0e = sb("w0e", [EF, 3, HID0])
        w0b = sb("w0b", [P, HC0, D])
        b2_0 = sb("b2_0", [P, D])
        bias0 = sb("bias0", [P, HC0])
        ident = sb("ident", [P, P])
        ones = sb("ones", [P, P])
        iota_f = sb("iota_f", [P, WIN])
        eps_col = sb("eps_col", [P, 1])
        epsilon = sb("epsilon", [P, 1])
        start = sb("start", [P, BLOCKS + 1])
        idx_f = sb("idx_f", [P, BLOCKS, FULL + 1])
        full_cap = sb("full_cap", [P, BLOCKS, FULL])
        tail_cap = sb("tail_cap", [P, BLOCKS, CHUNK])
        rinv = sb("rinv", [P, BLOCKS])
        has = sb("has", [P, BLOCKS])
        base_i = sb("base_i", [1, STEPS * GROUPS], I32)
        base_f = sb("base_f", [P, STEPS * GROUPS])
        flag = sb("flag", [1, 1], I32)
        out1T = sb("out1T", [EF, NPW])
        aggT = sb("aggT", [P, KC, NPW])
        onehot = [sb(f"onehot{j}", [P, TILES, WIN]) for j in range(2)]
        dst_t = [sb(f"dst_t{j}", [P, TILES], I32) for j in range(2)]
        w_t = [sb(f"w_t{j}", [P, TILES]) for j in range(2)]
        src_t = [sb(f"src_t{j}", [P, TILES], I32) for j in range(2)]
        dloc = sb("dloc", [P, TILES])
        hT = sb("hT", [P, HC0, P])
        xT_b = [sb(f"xT_b{j}", [P, KC, P]) for j in range(2)]
        xn_b = [sb(f"xn_b{j}", [P, D]) for j in range(2)]
        out_b = [sb(f"out_b{j}", [P, D]) for j in range(2)]
        z1 = sb("z1", [P, HID1])
        x2b = sb("x2b", [P, D])
        o1b = sb("o1b", [EF, P])
        o2b = sb("o2b", [EF, P])
        o3b = sb("o3b", [EF, P])
        rdiag = sb("rdiag", [P, P])
        chunk_max = sb("chunk_max", [P, FULL + 1, EF])
        max_w = sb("max_w", [P, EF])
        max_n = [sb(f"max_n{j}", [P, EF]) for j in range(2)]
        stats = sb("stats", [P, 6])
        mv = sb("mv", [P, 2])
        std = sb("std", [P, 1])
        rstd = sb("rstd", [P, 1])
        ell_idx = [sb(f"ell_idx{j}", [P, FULL + 1], I32) for j in range(2)]
        bad = sb("bad", [P, 4])
        bad_sum = sb("bad_sum", [P, 1])
        agg_in = sb("agg_in", [P, KC, P])

        ELL = SLOTS * EF
        NAT = TILES // 2 * EF
        ARENA = 2 * ELL + 2 * NAT
        arena = sb("arena", [P, ARENA])
        taken = [0]

        def piece(size, rows=P, dt=F32):
            lo = taken[0]
            taken[0] += -(-size // 8) * 8
            assert taken[0] <= ARENA
            v = arena[0:rows, lo:lo + size]
            return v if dt is F32 else v.bitcast(dt)

        ell = [piece(ELL) for j in range(2)]
        attr = [piece(NAT).rearrange("p (t f) -> p t f", f=EF) for j in range(2)]
        taken[0] = 0
        gath = [piece(COLS * D).rearrange("p (c d) -> p c d", d=D) for g in range(GROUPS)]
        after_gath = taken[0]
        w1T = piece(KC * HID1).rearrange("p (c h) -> p c h", c=KC)
        w2T = piece(HC1 * D).rearrange("p (c d) -> p c d", c=HC1)
        b1_1, g1_1, be1_1 = (piece(HID1) for _ in range(3))
        b2_1, g2_1, be2_1 = (piece(D) for _ in range(3))
        taken[0] = 0
        keys_i = piece(SPLIT, dt=I32)
        keys_f = piece(SPLIT)
        dn_i = piece(COLS_CHECK + 1, ROWS_CHECK, I32)
        dn_f = piece(COLS_CHECK, ROWS_CHECK)
        disorder = piece(COLS_CHECK, ROWS_CHECK)
        fine = [piece(SPLIT) for j in range(FINE_RING)]
        less = piece(SPLIT)
        w0u = piece(HID0, GF)
        u0 = piece(1, GF)
        b1_0 = piece(HC0)
        node_i = piece(BLOCKS, dt=I32)
        node_f = piece(BLOCKS)
        iota_i = piece(WIN, dt=I32)
        eights_i = piece(CHUNK, dt=I32)
        eights_f = piece(CHUNK)
        limit_i = piece(BLOCKS - 1, 1, I32)
        limit_f = piece(BLOCKS - 1, 1)
        base_b = piece(STEPS * GROUPS, dt=I32)
        ends_i = piece(STEPS * GROUPS, 1, I32)
        span_f = piece(STEPS * GROUPS, 1)
        coarse = piece(BLOCKS)
        row_i = piece(BLOCKS, dt=I32)
        in_row = piece(BLOCKS)
        shift = piece(P)
        wrap = piece(P)
        nxt = piece(BLOCKS)
        deg = piece(BLOCKS)
        full_f = piece(BLOCKS * FULL).rearrange("p (b j) -> p b j", j=FULL)
        n_full = piece(BLOCKS)
        tail_at = piece(BLOCKS)
        by_slot = piece(BLOCKS * CHUNK).rearrange("p (b j) -> p b j", j=CHUNK)
        late_f = piece(BLOCKS - 1, 1)
        taken[0] = 0
        out2T = piece(NP, EF)
        cntT = piece(NP, EF)
        g_attr = piece(EF)
        g_attrT = piece(P, EF)
        g_dst = piece(P, 1, I32)
        g_src = piece(1, dt=I32)
        g_w = piece(1)
        g_x = piece(D)
        g_xT = piece(KC * P).rearrange("p (c n) -> p c n", c=KC)
        g_one = piece(1, EF)

        seg = [bank("segA"), bank("segB")]
        hid = [bank("hidA"), bank("hidB")]
        zb = bank("zb")
        maxb = bank("maxb")
        x1b = bank("x1b")
        misc = bank("misc")

        keys_in, dn_in, win_in, u_in = sem("keys_in"), sem("dn_in"), sem("win_in"), sem("u_in")
        w0_in, eps_in, rows_out = sem("w0_in"), sem("eps_in"), sem("rows_out")
        fine_in = [sem(f"fine_in{j}") for j in range(FINE_RING)]
        dst_in = [sem(f"dst_in{j}") for j in range(2)]
        attr_in = [sem(f"attr_in{j}") for j in range(2)]
        ell_in = [sem(f"ell_in{j}") for j in range(2)]
        x_in = [sem(f"x_in{j}") for j in range(2)]
        x1_out = [sem(f"x1_out{j}") for j in range(2)]
        w1_in = sem("w1_in")
        edge_in = [sem(f"edge_in{j}") for j in range(2)]
        gath_in = [sem(f"gath_in{g}") for g in range(GROUPS)]
        x1_in = [sem(f"x1_in{j}") for j in range(2)]
        y_out = [sem(f"y_out{j}") for j in range(2)]
        consts_ready, dn_ready, count_ready = sem("consts_ready"), sem("dn_ready"), sem("count_ready")
        fine_used, start_ready, nxt_ps = sem("fine_used"), sem("start_ready"), sem("nxt_ps")
        bias_ps, bias_ready, bad_ready = sem("bias_ps"), sem("bias_ready"), sem("bad_ready")
        bad_ps, setup_done, ident_zero = sem("bad_ps"), sem("setup_done"), sem("ident_zero")
        ell_clear = sem("ell_clear")
        onehot_ready, seg_ps, seg_added = sem("onehot_ready"), sem("seg_ps"), sem("seg_added")
        ell_idx_ready, ell_used, max_ready = sem("ell_idx_ready"), sem("ell_used"), sem("max_ready")
        maxT_ps, rinv_ps, hid_ps, z_ps, x1T_ps = (
            sem("maxT_ps"), sem("rinv_ps"), sem("hid_ps"), sem("z_ps"), sem("x1T_ps"))
        rdiag_ready, o1_ready, o2_ready, relu_ready, std_ready, agg_init = (
            sem("rdiag_ready"), sem("o1_ready"), sem("o2_ready"), sem("relu_ready"),
            sem("std_ready"), sem("agg_init"))
        mean_ready, var_ready, x1_ready = sem("mean_ready"), sem("var_ready"), sem("x1_ready")
        wonehot_ready, msg_ps, msg_added = sem("wonehot_ready"), sem("msg_ps"), sem("msg_added")
        agg_ready, h1_ps, h1_ready, h1T_ps, h1T_ready, h2_ps = (
            sem("agg_ready"), sem("h1_ps"), sem("h1_ready"), sem("h1T_ps"), sem("h1T_ready"),
            sem("h2_ps"))
        var1_ready, std1_ready, y_ready = sem("var1_ready"), sem("std1_ready"), sem("y_ready")
        g_attr_in, g_dst_in, g_src_in, g_w_in, g_gath_in = (
            sem("g_attr_in"), sem("g_dst_in"), sem("g_src_in"), sem("g_w_in"), sem("g_gath_in"))
        g_turned, g_scaled, g_done, g_sums = (
            sem("g_turned"), sem("g_scaled"), sem("g_done"), sem("g_sums"))

        GT = EP // P
        block = ctx.enter_context(nc.Block())

        def is_fast(eng):
            eng.wait_ge(setup_done, 1)
            return eng.value_load(flag[0:1, 0:1], min_val=0, max_val=1) < 1

        @block.sync
        def _(sp):
            sp.dma_start(keys_i, t["keys"].partition_broadcast(P)).then_inc(keys_in, 16)
            sp.dma_start(dn_i, t["dst_rows"]).then_inc(dn_in, 16)
            sp.dma_start(base_b, t["base"].partition_broadcast(P)).then_inc(win_in, 16)
            sp.dma_start(base_i[:, :], t["base"].unsqueeze(0)).then_inc(win_in, 16)
            sp.dma_start(ends_i, t["ends"].unsqueeze(0)).then_inc(win_in, 16)
            sp.dma_start(w0u, t["W1"][D + 3 * EF:, :]).then_inc(u_in, 16)
            sp.dma_start(u0, t["u0"]).then_inc(u_in, 16)
            sp.dma_start(b1_0, t["b1_0"]).then_inc(u_in, 16)
            sp.dma_start(epsilon[:, :], t["epsilon"].to_broadcast([P, 1])).then_inc(eps_in, 16)
            sp.wait_ge(dn_ready, 1)
            sp.dma_start(dst_rows_d.rearrange("a b -> (a b)").rearrange("(p c) -> p c", c=COLS_CHECK),
                         dn_f).then_inc(rows_out, 16)
            sp.dma_start(w0x[:, :, :], t["W1"][0:D, :].rearrange("(c p) h -> p c h", p=P)).then_inc(w0_in, 16)
            sp.dma_start(w0e[:, :, :], t["W1"][D:D + 3 * EF, :].rearrange("(c p) h -> p c h", p=EF)).then_inc(w0_in, 16)
            sp.dma_start(w0b[:, :, :], t["W2"].rearrange("(c p) d -> p c d", p=P)).then_inc(w0_in, 16)
            sp.dma_start(b2_0[:, :], t["b2_0"].partition_broadcast(P)).then_inc(w0_in, 16)

            def load_x(m):
                wait(sp, z_ps, m.i - 1)
                wait(sp, var_ready, m.i - 1)
                sp.dma_start(xT_b[m.par][:, :, :], t["xT"].rearrange("(c p) n -> p c n", p=P)
                             [:, :, bass.ds(m.i * P, P)]).then_inc(x_in[m.par], 16)
                sp.dma_start(xn_b[m.par][:, :], t["x"][bass.ds(m.i * P, P), :]).then_inc(x_in[m.par], 16)

            def phase1(s, m):
                wait(sp, onehot_ready, s.i - 1)
                sp.dma_start(dst_t[s.par][:, :], t["dst_s"][bass.ds(s.i, 1), :, :]
                             .rearrange("a p t -> (a p) t")).then_inc(dst_in[s.par], 16)
                for half in range(2):
                    wait(sp, seg_ps, s.i * 2 - 1 + half)
                    rows = t["attr"].rearrange("(s g p c) f -> s p g (c f)", g=GROUPS, p=P, c=COLS)
                    sp.dma_start(attr[half].rearrange("p (g c) f -> p g (c f)", c=COLS),
                                 rows[bass.ds(s.i, 1), :, half * 4:half * 4 + 4, :]
                                 .rearrange("a p g r -> (a p) g r")).then_inc(attr_in[half], 16)
                if m is not None:
                    load_x(m)

            def load_second_layer():
                for out, name in ((w1T, "w1T"), (w2T, "w2T")):
                    sp.dma_start(out, t[name].rearrange("(c p) n -> p c n", p=P)).then_inc(w1_in, 16)
                for out, name in ((b1_1, "b1_1"), (g1_1, "g1_1"), (be1_1, "be1_1"),
                                  (b2_1, "b2_1"), (g2_1, "g2_1"), (be2_1, "be2_1")):
                    sp.dma_start(out, t[name].partition_broadcast(P)).then_inc(w1_in, 16)

            def all_x1(eng):
                for j in range(2):
                    eng.wait_ge(x1_out[j], 16 * ((BLOCKS + 1 - j) // 2))

            def load_x1(m):
                wait(sp, y_ready, m.i - 1)
                sp.dma_start(xn_b[m.par][:, :], x1_d[bass.ds(m.i * P, P), :]).then_inc(x1_in[m.par], 16)

            def phase2(s, m):
                wait(sp, msg_ps, (s.i - 1) * GROUPS)
                wait(sp, wonehot_ready, s.i - 1)
                for out, name in ((src_t, "src_s"), (dst_t, "dst_s"), (w_t, "w_s")):
                    sp.dma_start(out[s.par][:, :], t[name][bass.ds(s.i, 1), :, :]
                                 .rearrange("a p t -> (a p) t")).then_inc(edge_in[s.par], 16)
                if m is not None:
                    load_x1(m)

            with sp.If(is_fast(sp)):
                pipelined(sp, phase1, load_x)
                sp.wait_ge(ell_used, STEPS)
                sp.wait_ge(seg_ps, 2 * STEPS)
                load_second_layer()
                sp.wait_ge(var_ready, BLOCKS)
                all_x1(sp)
                pipelined(sp, phase2, load_x1)
            with sp.Else():
                with sp.Fori(0, GT) as k:
                    sp.wait_ge(g_done, k)
                    sp.dma_start(g_attr, t["attr"][bass.ds(k * P, P), :]).then_inc(g_attr_in, 16)
                    sp.dma_start(g_dst, t["dst_f"][bass.ds(k, 1), :]).then_inc(g_dst_in, 16)
                over_blocks(sp, load_x)
                all_x1(sp)
                with sp.Fori(0, GT) as k:
                    sp.wait_ge(g_done, k + GT)
                    sp.dma_start(g_src, t["src_f"][bass.ds(k * P, P), :]).then_inc(g_src_in, 16)
                    sp.dma_start(g_w, t["w_f"][bass.ds(k * P, P), :]).then_inc(g_w_in, 16)
                    sp.dma_start(g_dst, t["dst_f"][bass.ds(k, 1), :]).then_inc(g_dst_in, 16)
                sp.wait_ge(g_done, 2 * GT)
                load_second_layer()
                over_blocks(sp, load_x1)

        @block.gpsimd
        def _(pool):
            pool.iota(node_i, pattern=[[P, BLOCKS]], base=0, channel_multiplier=1).then_inc(consts_ready, 1)
            pool.iota(iota_i, pattern=[[1, WIN]], base=0, channel_multiplier=0).then_inc(consts_ready, 1)
            pool.iota(eights_i, pattern=[[CHUNK, CHUNK]], base=0, channel_multiplier=0).then_inc(consts_ready, 1)
            pool.iota(limit_i, pattern=[[STEP, BLOCKS - 1]], base=2 * STEP, channel_multiplier=0).then_inc(consts_ready, 1)
            pool.memset(ident[:, :], 0.0).then_inc(ident_zero, 1)
            pool.memset(shift, 0.0).then_inc(ident_zero, 1)
            pool.memset(wrap, 0.0).then_inc(ident_zero, 1)
            pool.wait_ge(ident_zero, 3)
            pool.affine_select(out=ident[:, :], in_=ident[:, :], compare_op=ALU.not_equal, fill=1.0,
                               base=0, pattern=[[-1, P]], channel_multiplier=1).then_inc(consts_ready, 1)
            pool.affine_select(out=shift, in_=shift, compare_op=ALU.not_equal, fill=1.0,
                               base=-1, pattern=[[-1, P]], channel_multiplier=1).then_inc(consts_ready, 1)
            pool.memset(wrap[0:1, P - 1:P], 1.0).then_inc(consts_ready, 1)
            pool.memset(ones[:, :], 1.0).then_inc(consts_ready, 1)
            pool.memset(eps_col[:, :], LN_EPS).then_inc(consts_ready, 1)
            pool.wait_ge(rows_out, 16)
            for b in range(BLOCKS):
                pool.wait_ge(count_ready, b + 1)
                if b >= FINE_RING:
                    pool.wait_ge(fine_used, b - FINE_RING + 1)
                pool.indirect_dma_start(fine[b % FINE_RING], None, dst_rows_d,
                                        bass.IndirectOffsetOnAxis(ap=row_i[:, b:b + 1], axis=0),
                                        bounds_check=SPLIT - 1, oob_is_err=False
                                        ).then_inc(fine_in[b % FINE_RING], 16)

            bound = pool.alloc_register("bound")

            def wait_for_bound(sem_, value, last_row):
                wait(pool, sem_, value)
                pool.reg_alu(bound, bound, last_row, ALU.min)
                return pool.snap(bound, min_val=0, max_val=last_row)

            def phase1(s, m):
                wait(pool, ell_used, s.i - 1)
                pool.tensor_copy(ell_idx[s.par][:, :], idx_f[:, bass.ds(s.i, 1), :]
                                 .rearrange("p a j -> p (a j)")).then_inc(ell_idx_ready, 1)
                last_row = wait_for_bound(ell_idx_ready, s.i + 1, EP - CHUNK)
                for j in range(FULL + 1):
                    pool.indirect_dma_start(ell[s.par][:, j * CHUNK * EF:(j + 1) * CHUNK * EF], None,
                                            t["attr"], bass.IndirectOffsetOnAxis(
                                                ap=ell_idx[s.par][:, j:j + 1], axis=0),
                                            bounds_check=last_row, oob_is_err=False
                                            ).then_inc(ell_in[s.par], 16)

            def phase2(s, m):
                pool.wait_ge(edge_in[s.par], s.uses * 48 + 48)
                for g in range(GROUPS):
                    last_row = wait_for_bound(msg_ps, (s.i - 1) * GROUPS + g + 1, NP - 1)
                    for c in range(COLS):
                        pool.indirect_dma_start(gath[g][:, c, :], None, x1_d,
                                                bass.IndirectOffsetOnAxis(
                                                    ap=src_t[s.par][:, g * COLS + c:g * COLS + c + 1], axis=0),
                                                bounds_check=last_row, oob_is_err=False
                                                ).then_inc(gath_in[g], 16)

            def all_x1():
                for j in range(2):
                    pool.wait_ge(x1_out[j], 16 * ((BLOCKS + 1 - j) // 2))

            pool.reg_mov(bound, EP)
            with pool.If(is_fast(pool)):
                for j in range(2):
                    pool.memset(ell[j], 0.0).then_inc(ell_clear, 1)
                pool.wait_ge(ell_clear, 2)
                pipelined(pool, phase1, lambda m: None)
                all_x1()
                pool.wait_ge(ell_used, STEPS)
                pool.wait_ge(seg_ps, 2 * STEPS)
                pipelined(pool, phase2, lambda m: None)
            with pool.Else():
                all_x1()
                with pool.Fori(0, GT) as k:
                    last_row = wait_for_bound(g_src_in, k * 16 + 16, NP - 1)
                    pool.indirect_dma_start(g_x, None, x1_d, bass.IndirectOffsetOnAxis(ap=g_src, axis=0),
                                            bounds_check=last_row, oob_is_err=False).then_inc(g_gath_in, 16)
                    pool.wait_ge(g_gath_in, k * 16 + 16)

        @block.tensor
        def _(pe):
            pe.wait_ge(consts_ready, 9)
            pe.wait_ge(u_in, 48)
            for c in range(HC0):
                mm = pe.matmul(misc[:, c:c + 1], w0u[:, c * P:(c + 1) * P], u0, start=True, stop=True)
            mm.then_inc(bias_ps, 1)
            pe.wait_ge(start_ready, 1)
            pe.matmul(zb[:, 0:BLOCKS], shift, start[:, 0:BLOCKS], start=True, stop=False)
            pe.matmul(zb[:, 0:BLOCKS], wrap, start[:, 1:BLOCKS + 1], start=False, stop=True).then_inc(nxt_ps, 1)
            pe.wait_ge(bad_ready, 1)
            pe.matmul(maxb[0:1, 0:1], bad_sum[:, :], ones[:, 0:1], start=True, stop=True).then_inc(bad_ps, 1)
            pe.wait_ge(w0_in, 64)

            def sums(s):
                pe.wait_ge(onehot_ready, s.i + 1)
                for half in range(2):
                    pe.wait_ge(attr_in[half], s.i * 16 + 16)
                    wait(pe, seg_added, s.i * 2 - 1 + half)
                    for g in range(GROUPS // 2):
                        for c in range(COLS):
                            mm = pe.matmul(seg[half][0:EF, g * WIN:(g + 1) * WIN], attr[half][:, g * COLS + c, :],
                                           onehot[s.par][:, half * 16 + g * COLS + c, :],
                                           start=(c == 0), stop=(c == COLS - 1))
                    mm.then_inc(seg_ps, 1)

            def hidden(m, parts, first, last):
                for half in range(2):
                    for c in range(HC0 // 2):
                        h = half * (HC0 // 2) + c
                        for n, (w, x) in enumerate(parts):
                            mm = pe.matmul(hid[half][:, c * P:(c + 1) * P], w[:, h * P:(h + 1) * P], x,
                                           start=(first and c == 0 and n == 0),
                                           stop=(last and n == len(parts) - 1), skip_group_check=True)
                    if last:
                        mm.then_inc(hid_ps, 1)

            def turn_x1(m):
                pe.wait_ge(x1_ready, m.i + 1)
                wait(pe, agg_init, m.i)
                for c in range(KC):
                    mm = pe.transpose(x1b[:, c * P:(c + 1) * P], out_b[m.par][:, c * P:(c + 1) * P], ident[:, :])
                mm.then_inc(x1T_ps, 1)

            def mlp0(m, fast):
                wait(pe, relu_ready, m.i * 2)
                pe.wait_ge(x_in[m.par], m.uses * 32 + 32)
                hidden(m, [(w0x[:, k, :], xT_b[m.par][:, k, :]) for k in range(KC)], True, False)
                if not m.first():
                    turn_x1(m.before())
                if fast:
                    pe.wait_ge(max_ready, m.i + 1)
                    wait(pe, o2_ready, m.i)
                    pe.transpose(maxb[0:EF, 0:P], max_n[m.par][:, :], ident[:, :]).then_inc(maxT_ps, 1)
                    pe.wait_ge(rdiag_ready, m.i + 1)
                    wait(pe, mean_ready, m.i)
                    pe.matmul(misc[0:EF, 0:P], ones[:, 0:EF], rdiag[:, :], start=True, stop=True).then_inc(rinv_ps, 1)
                pe.wait_ge(o1_ready, m.i + 1)
                pe.wait_ge(o2_ready, m.i + 1)
                pe.wait_ge(mean_ready, m.i + 1)
                hidden(m, [(w0e[:, 0, :], o1b[:, :]), (w0e[:, 1, :], o2b[:, :]), (w0e[:, 2, :], o3b[:, :])],
                       False, True)
                wait(pe, var_ready, m.i)
                for c in range(HC0):
                    if c % (HC0 // 2) == 0:
                        pe.wait_ge(relu_ready, m.i * 2 + 1 + c // (HC0 // 2))
                    mm = pe.matmul(zb[:, 0:D], hT[:, c, :], w0b[:, c, :], start=(c == 0), stop=(c == HC0 - 1))
                mm.then_inc(z_ps, 1)

            def phase1(s, m):
                sums(s)
                if m is not None:
                    mlp0(m, True)

            def messages(s):
                pe.wait_ge(wonehot_ready, s.i + 1)
                for g in range(GROUPS):
                    half, q = g // 4, g % 4
                    if q == 0:
                        wait(pe, msg_added, s.i * 2 - 1 + half)
                    pe.wait_ge(gath_in[g], s.i * 16 * COLS + 16 * COLS)
                    for k in range(KC):
                        for c in range(COLS):
                            lo = (q * KC + k) * WIN
                            mm = pe.matmul(seg[half][:, lo:lo + WIN], gath[g][:, c, k * P:(k + 1) * P],
                                           onehot[s.par][:, g * COLS + c, :],
                                           start=(c == 0), stop=(c == COLS - 1))
                    mm.then_inc(msg_ps, 1)

            def mlp1(m):
                pe.wait_ge(agg_ready, m.i + 1)
                wait(pe, var1_ready, m.i * 3 - 2)
                for k in range(KC):
                    mm = pe.matmul(hid[0][:, :], agg_in[:, k, :], w1T[:, k, :], start=(k == 0), stop=(k == KC - 1))
                mm.then_inc(h1_ps, 1)
                pe.wait_ge(h1_ready, m.i + 1)
                wait(pe, h1T_ready, m.i)
                for c in range(HC1):
                    mm = pe.transpose(hid[1][:, c * P:(c + 1) * P], z1[:, c * P:(c + 1) * P], ident[:, :])
                mm.then_inc(h1T_ps, 1)
                pe.wait_ge(h1T_ready, m.i + 1)
                wait(pe, var1_ready, m.i * 3 - 1)
                for c in range(HC1):
                    mm = pe.matmul(zb[:, 0:D], hT[:, c, :], w2T[:, c, :], start=(c == 0), stop=(c == HC1 - 1))
                mm.then_inc(h2_ps, 1)

            def phase2(s, m):
                messages(s)
                if m is not None:
                    mlp1(m)

            with pe.If(is_fast(pe)):
                pipelined(pe, phase1, lambda m: mlp0(m, True))
                turn_x1(at(BLOCKS - 1))
                pe.wait_ge(w1_in, 16 * 8)
                pipelined(pe, phase2, mlp1)
            with pe.Else():
                with pe.Fori(0, GT) as k:
                    pe.wait_ge(g_attr_in, k * 16 + 16)
                    pe.transpose(misc[0:EF, 0:P], g_attr, ident[:, :]).then_inc(g_turned, 1)
                over_blocks(pe, lambda m: mlp0(m, False))
                turn_x1(at(BLOCKS - 1))
                with pe.Fori(0, GT) as k:
                    pe.wait_ge(g_scaled, k + 1)
                    for c in range(KC):
                        mm = pe.transpose(misc[:, c * P:(c + 1) * P], g_x[:, c * P:(c + 1) * P], ident[:, :])
                    mm.then_inc(g_turned, 1)
                pe.wait_ge(w1_in, 16 * 8)
                over_blocks(pe, mlp1)

        @block.scalar
        def _(act):
            def turned_x1(m):
                act.wait_ge(x1T_ps, m.i + 1)
                act.activation(aggT[:, :, bass.ds(m.i * P, P)], x1b[:, 0:D].rearrange("p (c n) -> p c n", c=KC),
                               ACT.Copy, scale=epsilon[:, 0:1]).then_inc(agg_init, 1)

            def deviation(m, have, want, n=0, per=1):
                act.wait_ge(have, m.i * per + n + 1)
                act.activation(std[:, :], mv[:, 1:2], ACT.Sqrt, bias=eps_col[:, 0:1]).then_inc(want, 1)

            def mlp0(m, fast):
                if fast:
                    wait(act, rinv_ps, m.i)
                    act.activation(rdiag[:, :], ident[:, :], ACT.Copy,
                                   scale=rinv[:, bass.ds(m.i, 1)]).then_inc(rdiag_ready, 1)
                if not m.first():
                    turned_x1(m.before())
                if fast:
                    act.wait_ge(seg_added, 2 * STEPS if m.last() else m.i * 2 + 4)
                wait(act, hid_ps, m.i * 2)
                wait(act, mean_ready, m.i)
                act.activation(o1b[:, :], out1T[:, bass.ds(m.i * P, P)], ACT.Copy).then_inc(o1_ready, 1)
                if fast:
                    act.wait_ge(maxT_ps, m.i + 1)
                    act.activation(o2b[:, :], maxb[0:EF, 0:P], ACT.Copy).then_inc(o2_ready, 1)
                else:
                    act.activation(o2b[:, :], out2T[:, bass.ds(m.i * P, P)], ACT.Copy).then_inc(o2_ready, 1)
                wait(act, z_ps, m.i)
                for c in range(HC0):
                    half, q = c // (HC0 // 2), c % (HC0 // 2)
                    if q == 0:
                        act.wait_ge(hid_ps, m.i * 2 + 1 + half)
                    relu = act.activation(hT[:, c, :], hid[half][:, q * P:(q + 1) * P], ACT.Relu,
                                          bias=bias0[:, c:c + 1])
                    if q == HC0 // 2 - 1:
                        relu.then_inc(relu_ready, 1)
                deviation(m, var_ready, std_ready)
                act.wait_ge(x1_ready, m.i + 1)
                act.dma_start(x1_d[bass.ds(m.i * P, P), :], out_b[m.par][:, :]).then_inc(x1_out[m.par], 16)

            def mlp1(m, fast):
                if fast:
                    act.wait_ge(msg_added, 2 * STEPS if m.last() else m.i * 2 + 4)
                wait(act, h1_ps, m.i)
                act.activation(agg_in[:, :, :], aggT[:, :, bass.ds(m.i * P, P)], ACT.Copy).then_inc(agg_ready, 1)
                deviation(m, var1_ready, std1_ready, 0, 3)
                act.wait_ge(h1T_ps, m.i + 1)
                wait(act, h2_ps, m.i)
                act.activation(hT[:, 0:HC1, :], hid[1][:, :].rearrange("p (c n) -> p c n", c=HC1),
                               ACT.Relu).then_inc(h1T_ready, 1)
                deviation(m, var1_ready, std1_ready, 1, 3)
                deviation(m, var1_ready, std1_ready, 2, 3)
                act.wait_ge(y_ready, m.i + 1)
                act.dma_start(t["y"][bass.ds(m.i * P, P), :], out_b[m.par][:, :]).then_inc(y_out[m.par], 16)

            act.wait_ge(eps_in, 16)
            with act.If(is_fast(act)):
                pipelined(act, lambda s, m: m is not None and mlp0(m, True), lambda m: mlp0(m, True))
                turned_x1(at(BLOCKS - 1))
                pipelined(act, lambda s, m: m is not None and mlp1(m, True), lambda m: mlp1(m, True))
            with act.Else():
                act.wait_ge(g_sums, 1)
                over_blocks(act, lambda m: mlp0(m, False))
                turned_x1(at(BLOCKS - 1))
                act.wait_ge(g_done, 2 * GT)
                over_blocks(act, lambda m: mlp1(m, False))
            for j in range(2):
                act.wait_ge(y_out[j], 16 * ((BLOCKS + 1 - j) // 2))

        @block.vector
        def _(dve):
            tt, ts, red = dve.tensor_tensor, dve.tensor_scalar, dve.tensor_reduce

            def settle():
                dve.drain()

            dve.memset(start[:, BLOCKS:BLOCKS + 1], float(EP))
            dve.memset(bad[:, :], 0.0)
            dve.memset(out1T[:, :], 0.0)
            dve.memset(aggT[:, :, NP:NPW], 0.0)
            dve.wait_ge(dn_in, 16)
            dve.tensor_copy(dn_f, dn_i[:, 0:COLS_CHECK]).then_inc(dn_ready, 1)
            dve.wait_ge(keys_in, 16)
            dve.tensor_copy(keys_f, keys_i)
            dve.wait_ge(consts_ready, 9)
            dve.tensor_copy(node_f, node_i)
            settle()
            lag = FINE_RING - 2
            for b in range(BLOCKS + lag):
                if b < BLOCKS:
                    ts(less, keys_f, node_f[:, b:b + 1], None, ALU.is_lt, ALU.add, accum_out=coarse[:, b:b + 1])
                    settle()
                    ts(row_i[:, b:b + 1], coarse[:, b:b + 1], -1.0, 0.0, ALU.add, ALU.max).then_inc(count_ready, 1)
                if b >= lag:
                    d = b - lag
                    dve.wait_ge(fine_in[d % FINE_RING], 16 * (d // FINE_RING + 1))
                    ts(less, fine[d % FINE_RING], node_f[:, d:d + 1], None, ALU.is_lt, ALU.add,
                       accum_out=in_row[:, d:d + 1]).then_inc(fine_used, 1)
                    settle()
            ts(coarse, coarse, -1.0, 0.0, ALU.add, ALU.max)
            settle()
            dve.scalar_tensor_tensor(out=start[:, 0:BLOCKS], in0=coarse, scalar=float(SPLIT), in1=in_row,
                                     op0=ALU.mult, op1=ALU.add).then_inc(start_ready, 1)

            tt(disorder, dn_i[:, 0:COLS_CHECK], dn_i[:, 1:COLS_CHECK + 1], ALU.is_gt)
            dve.wait_ge(win_in, 48)
            tt(span_f, ends_i, base_i[:, :], ALU.subtract)
            dve.tensor_copy(base_f[:, :], base_b)
            dve.tensor_copy(iota_f[:, :], iota_i)
            dve.tensor_copy(eights_f, eights_i)
            dve.tensor_copy(limit_f, limit_i)
            settle()
            red(bad[0:ROWS_CHECK, 0:1], disorder, AX.X, ALU.add)
            ts(span_f, span_f, float(WIN), None, ALU.is_ge)
            tt(late_f, start[0:1, 1:BLOCKS], limit_f, ALU.is_gt)
            settle()
            red(bad[0:1, 1:2], span_f, AX.X, ALU.add)
            red(bad[0:1, 2:3], late_f, AX.X, ALU.add)

            dve.wait_ge(nxt_ps, 1)
            dve.tensor_copy(nxt, zb[:, 0:BLOCKS])
            settle()
            tt(deg, nxt, start[:, 0:BLOCKS], ALU.subtract)
            settle()
            ts(n_full, deg, float(SLOTS), None, ALU.is_gt)
            tt(full_f, deg.unsqueeze(2).to_broadcast([P, BLOCKS, FULL]),
               eights_f[:, 1:CHUNK].unsqueeze(1).to_broadcast([P, BLOCKS, FULL]), ALU.is_gt)
            ts(rinv[:, :], deg, 1.0, None, ALU.max)
            ts(has[:, :], deg, 1.0, None, ALU.min)
            settle()
            red(bad[:, 3:4], n_full, AX.X, ALU.add)
            dve.reciprocal(rinv[:, :], rinv[:, :])
            ts(full_cap[:, :, :], full_f, 0.5, 2.0, ALU.subtract, ALU.mult)
            settle()
            red(bad_sum[:, :], bad[:, :], AX.X, ALU.add).then_inc(bad_ready, 1)
            red(n_full, full_f, AX.X, ALU.add)
            ts(full_cap[:, :, :], full_cap[:, :, :], BIG, None, ALU.mult)
            tt(idx_f[:, :, 0:FULL], start[:, 0:BLOCKS].unsqueeze(2).to_broadcast([P, BLOCKS, FULL]),
               eights_f[:, 0:FULL].unsqueeze(1).to_broadcast([P, BLOCKS, FULL]), ALU.add)
            settle()
            ts(full_f, full_f, -SKIP, SKIP, ALU.mult, ALU.add)
            settle()
            tt(idx_f[:, :, 0:FULL], idx_f[:, :, 0:FULL], full_f, ALU.add)
            dve.scalar_tensor_tensor(out=tail_at, in0=n_full, scalar=float(CHUNK), in1=start[:, 0:BLOCKS],
                                     op0=ALU.mult, op1=ALU.add)
            settle()
            ts(idx_f[:, :, FULL:FULL + 1], tail_at.unsqueeze(2), float(EP - CHUNK), None, ALU.min)
            settle()
            ts(eights_f, eights_f, 1.0 / CHUNK, None, ALU.mult)
            settle()
            tt(by_slot, idx_f[:, :, FULL:FULL + 1].to_broadcast([P, BLOCKS, CHUNK]),
               eights_f.unsqueeze(1).to_broadcast([P, BLOCKS, CHUNK]), ALU.add)
            settle()
            tt(tail_cap[:, :, :], by_slot, tail_at.unsqueeze(2).to_broadcast([P, BLOCKS, CHUNK]), ALU.is_ge)
            tt(by_slot, by_slot, nxt.unsqueeze(2).to_broadcast([P, BLOCKS, CHUNK]), ALU.is_lt)
            settle()
            tt(tail_cap[:, :, :], tail_cap[:, :, :], by_slot, ALU.mult)
            settle()
            ts(tail_cap[:, :, :], tail_cap[:, :, :], 0.5, 2.0, ALU.subtract, ALU.mult)
            settle()
            ts(tail_cap[:, :, :], tail_cap[:, :, :], BIG, None, ALU.mult)
            dve.wait_ge(bias_ps, 1)
            tt(bias0[:, :], misc[:, 0:HC0], b1_0, ALU.add)
            dve.wait_ge(bad_ps, 1)
            ts(flag[:, :], maxb[0:1, 0:1], 1.0, None, ALU.min)
            settle()
            dve.memset(mv[:, :], 0.0).then_inc(setup_done, 1)

            base_regs = [dve.alloc_register(f"base{g}") for g in range(GROUPS)]

            def load_bases(s):
                dve.load(base_regs, base_i[0:1, bass.ds(s.i * GROUPS, GROUPS)])
                return [dve.snap(r, min_val=0, max_val=NP - 1) for r in base_regs]

            def window_matrix(s, weighted):
                if weighted:
                    dve.wait_ge(edge_in[s.par], s.uses * 48 + 48)
                    wait(dve, msg_ps, (s.i - 1) * GROUPS)
                else:
                    dve.wait_ge(dst_in[s.par], s.uses * 16 + 16)
                    wait(dve, seg_ps, (s.i - 1) * 2)
                tt(dloc[:, :].rearrange("p (g c) -> p g c", c=COLS),
                   dst_t[s.par][:, :].rearrange("p (g c) -> p g c", c=COLS),
                   base_f[:, bass.ds(s.i * GROUPS, GROUPS)].unsqueeze(2).to_broadcast([P, GROUPS, COLS]),
                   ALU.subtract)
                settle()
                eq = tt(onehot[s.par][:, :, :], dloc[:, :].unsqueeze(2).to_broadcast([P, TILES, WIN]),
                        iota_f[:, :].unsqueeze(1).to_broadcast([P, TILES, WIN]), ALU.is_equal)
                if weighted:
                    settle()
                    tt(onehot[s.par][:, :, :], onehot[s.par][:, :, :],
                       w_t[s.par][:, :].unsqueeze(2).to_broadcast([P, TILES, WIN]),
                       ALU.mult).then_inc(wonehot_ready, 1)
                else:
                    eq.then_inc(onehot_ready, 1)
                settle()

            def add_sums(s):
                bases = load_bases(s)
                for g in range(GROUPS):
                    half, q = g // 4, g % 4
                    if q == 0:
                        dve.wait_ge(seg_ps, s.i * 2 + 1 + half)
                    to = out1T[:, bass.ds(bases[g], WIN)]
                    add = tt(to, to, seg[half][0:EF, q * WIN:(q + 1) * WIN], ALU.add)
                    if q == 3:
                        add.then_inc(seg_added, 1)
                    settle()

            def add_messages(s):
                bases = load_bases(s)
                for g in range(GROUPS):
                    half, q = g // 4, g % 4
                    if q == 0:
                        dve.wait_ge(msg_ps, s.i * GROUPS + g + 4)
                    to = aggT[:, :, bass.ds(bases[g], WIN)]
                    add = tt(to, to, seg[half][:, q * KC * WIN:(q + 1) * KC * WIN]
                             .rearrange("p (c n) -> p c n", c=KC), ALU.add)
                    if q == 3:
                        add.then_inc(msg_added, 1)
                    settle()

            def maxima(s):
                dve.wait_ge(ell_in[s.par], s.uses * 16 * (FULL + 1) + 16 * (FULL + 1))
                tail = ell[s.par][:, FULL * CHUNK * EF:].rearrange("p (k f) -> p k f", f=EF)
                tt(tail, tail, tail_cap[:, bass.ds(s.i, 1), :].rearrange("p a k -> p (a k)")
                   .unsqueeze(2).to_broadcast([P, CHUNK, EF]), ALU.min)
                settle()
                red(chunk_max[:, :, :], ell[s.par].rearrange("p (j k f) -> p j f k", k=CHUNK, f=EF),
                    AX.X, ALU.max).then_inc(ell_used, 1)
                settle()
                tt(chunk_max[:, 0:FULL, :], chunk_max[:, 0:FULL, :],
                   full_cap[:, bass.ds(s.i, 1), :].rearrange("p a j -> p (a j)")
                   .unsqueeze(2).to_broadcast([P, FULL, EF]), ALU.min)
                settle()
                red(max_w[:, :], chunk_max[:, :, :].rearrange("p j f -> p f j"), AX.X, ALU.max)
                settle()
                wait(dve, maxT_ps, s.i - 1)
                ts(max_n[s.par][:, :], max_w[:, :], has[:, bass.ds(s.i, 1)], None, ALU.mult).then_inc(max_ready, 1)

            def mean(m, fast):
                dve.wait_ge(o1_ready, m.i + 1)
                wait(dve, hid_ps, m.i * 2)
                if fast:
                    dve.wait_ge(rinv_ps, m.i + 1)
                    by = misc[0:EF, 0:P]
                else:
                    by = cntT[:, bass.ds(m.i * P, P)]
                tt(o3b[:, :], o1b[:, :], by, ALU.mult).then_inc(mean_ready, 1)

            def moments(v, ready):
                settle()
                dve.bn_stats(stats[:, :], v)
                settle()
                dve.bn_aggr(mv[:, :], stats[:, :]).then_inc(ready, 1)

            def normed(out, v, ready, count):
                dve.wait_ge(ready, count)
                dve.reciprocal(rstd[:, :], std[:, :])
                settle()
                return ts(out, v, mv[:, 0:1], rstd[:, 0:1], ALU.subtract, ALU.mult)

            def norm0(m):
                dve.wait_ge(x_in[m.par], m.uses * 32 + 32)
                dve.scalar_tensor_tensor(out=x2b[:, :], in0=xn_b[m.par][:, :], scalar=2.0, in1=b2_0[:, :],
                                         op0=ALU.mult, op1=ALU.add)
                settle()
                dve.wait_ge(z_ps, m.i + 1)
                tt(z1[:, 0:D], zb[:, 0:D], x2b[:, :], ALU.add)
                moments(z1[:, 0:D], var_ready)
                wait(dve, x1_out[m.par], m.uses * 16)
                wait(dve, x1T_ps, m.i - 1)
                normed(out_b[m.par][:, :], z1[:, 0:D], std_ready, m.i + 1).then_inc(x1_ready, 1)

            def norm1(m):
                dve.wait_ge(h1_ps, m.i + 1)
                wait(dve, h1T_ps, m.i)
                tt(z1[:, :], hid[0][:, :], b1_1, ALU.add)
                moments(z1[:, :], var1_ready)
                normed(z1[:, :], z1[:, :], std1_ready, m.i * 3 + 1)
                settle()
                tt(z1[:, :], z1[:, :], g1_1, ALU.mult)
                settle()
                tt(z1[:, :], z1[:, :], be1_1, ALU.add).then_inc(h1_ready, 1)
                y = x2b[:, :]
                dve.wait_ge(h2_ps, m.i + 1)
                tt(y, zb[:, 0:D], b2_1, ALU.add)
                moments(y, var1_ready)
                normed(y, y, std1_ready, m.i * 3 + 2)
                settle()
                tt(y, y, g2_1, ALU.mult)
                settle()
                tt(y, y, be2_1, ALU.add)
                settle()
                dve.wait_ge(x1_in[m.par], m.uses * 16 + 16)
                dve.scalar_tensor_tensor(out=y, in0=y, scalar=0.0, in1=xn_b[m.par][:, :],
                                         op0=ALU.max, op1=ALU.add)
                moments(y, var1_ready)
                wait(dve, y_out[m.par], m.uses * 16)
                normed(out_b[m.par][:, :], y, std1_ready, m.i * 3 + 3).then_inc(y_ready, 1)

            def phase1(s, m):
                add_sums(s)
                if not s.last():
                    window_matrix(s.next(), False)
                if m is not None:
                    mean(m, True)
                maxima(s)
                if m is not None:
                    norm0(m)

            def last1(m):
                mean(m, True)
                norm0(m)

            def phase2(s, m):
                add_messages(s)
                if not s.last():
                    window_matrix(s.next(), True)
                if m is not None:
                    norm1(m)

            def edge_by_edge(k, from_ps, to, add):
                dve.wait_ge(g_dst_in, k * 16 + 16)
                dve.tensor_copy(to, from_ps)
                settle()
                with dve.Fori(0, P) as e:
                    node = dve.value_load(g_dst[0:1, bass.ds(e, 1)], min_val=0, max_val=NP - 1)
                    add(node, e)
                    settle()
                dve.memset(rstd[:, :], 0.0).then_inc(g_done, 1)
                settle()

            def sum_and_max(node, e):
                row = g_attrT[:, bass.ds(e, 1)]
                tt(out1T[:, bass.ds(node, 1)], out1T[:, bass.ds(node, 1)], row, ALU.add)
                tt(out2T[:, bass.ds(node, 1)], out2T[:, bass.ds(node, 1)], row, ALU.max)
                tt(cntT[:, bass.ds(node, 1)], cntT[:, bass.ds(node, 1)], g_one, ALU.add)

            def add_message(node, e):
                to = aggT[:, :, bass.ds(node, 1)]
                tt(to, to, g_xT[:, :, bass.ds(e, 1)], ALU.add)

            with dve.If(is_fast(dve)):
                window_matrix(at(0), False)
                pipelined(dve, phase1, last1)
                dve.wait_ge(agg_init, BLOCKS)
                dve.wait_ge(w1_in, 16 * 8)
                window_matrix(at(0), True)
                pipelined(dve, phase2, norm1)
            with dve.Else():
                dve.memset(out2T, -BIG)
                dve.memset(cntT, 0.0)
                dve.memset(g_one, 1.0)
                settle()
                with dve.Fori(0, GT) as k:
                    dve.wait_ge(g_turned, k + 1)
                    edge_by_edge(k, misc[0:EF, 0:P], g_attrT, sum_and_max)
                ts(g_one, g_one, 1.0, None, ALU.mult)
                settle()
                dve.scalar_tensor_tensor(out=out2T, in0=cntT, scalar=1.0, in1=out2T, op0=ALU.min, op1=ALU.mult)
                settle()
                ts(cntT, cntT, 1.0, None, ALU.max)
                settle()
                dve.reciprocal(cntT, cntT).then_inc(g_sums, 1)
                settle()

                def one(m):
                    mean(m, False)
                    norm0(m)

                over_blocks(dve, one)
                dve.wait_ge(agg_init, BLOCKS)
                with dve.Fori(0, GT) as k:
                    dve.wait_ge(g_gath_in, k * 16 + 16)
                    dve.wait_ge(g_w_in, k * 16 + 16)
                    ts(g_x, g_x, g_w[:, 0:1], None, ALU.mult).then_inc(g_scaled, 1)
                    dve.wait_ge(g_turned, k + GT + 1)
                    edge_by_edge(k + GT, misc[:, 0:D].rearrange("p (c n) -> p c n", c=KC), g_xT, add_message)
                dve.wait_ge(w1_in, 16 * 8)
                over_blocks(dve, norm1)


def kernel(**a):
    from concourse import bacc
    from concourse.bass_utils import run_bass_kernel_spmd

    pad_e, pad_n = EP - N_EDGES, NP - N_NODES
    a = {k: np.asarray(v) for k, v in a.items()}
    pad_dst = np.repeat(np.arange(N_NODES, NP, dtype=np.int32), PAD_DEG)
    src = np.concatenate([a["src"], np.zeros(pad_e, np.int32)])
    dst = np.concatenate([a["dst"], pad_dst])
    weight = np.concatenate([a["edge_weight"], np.zeros(pad_e, np.float32)])
    attr = np.concatenate([a["edge_attr_96"], np.zeros((pad_e, EF), np.float32)])
    x = np.concatenate([a["x"], np.zeros((pad_n, D), np.float32)])

    def by_step(v):
        return v.reshape(STEPS, GROUPS, P, COLS).transpose(0, 2, 1, 3).reshape(STEPS, P, TILES)

    past = np.concatenate([dst, np.full(1, NP, np.int32)])
    arrays = {
        "attr": attr, "x": x, "xT": x.T,
        "src_s": by_step(src), "dst_s": by_step(dst), "w_s": by_step(weight),
        "src_f": src.reshape(EP, 1), "w_f": weight.reshape(EP, 1), "dst_f": dst.reshape(EP // P, P),
        "keys": dst[::SPLIT], "base": dst[::GROUP], "ends": dst[GROUP - 1::GROUP],
        "dst_rows": np.concatenate([dst.reshape(ROWS_CHECK, COLS_CHECK),
                                    past[COLS_CHECK::COLS_CHECK].reshape(ROWS_CHECK, 1)], axis=1),
        "W1": a["L0_gnn_W1"], "W2": a["L0_gnn_W2"], "b1_0": a["L0_gnn_b1"].reshape(HC0, P).T,
        "b2_0": a["L0_gnn_b2"], "u0": a["L0_gnn_u"][0].reshape(GF, 1), "epsilon": a["L1_gnn_epsilon"],
        "w1T": a["L1_gnn_w1"].T, "w2T": a["L1_gnn_w2"].T,
        "b1_1": a["L1_gnn_b1"], "g1_1": a["L1_gnn_g1"], "be1_1": a["L1_gnn_beta1"],
        "b2_1": a["L1_gnn_b2"], "g2_1": a["L1_gnn_g2"], "be2_1": a["L1_gnn_beta2"],
    }
    arrays = {k + "_in": np.ascontiguousarray(v) for k, v in arrays.items()}
    nc = bacc.Bacc("TRN2", target_bir_lowering=False, num_devices=1)
    t = {k[:-3]: nc.dram_tensor(k, v.shape, mybir.dt.from_np(v.dtype), kind="ExternalInput").ap()
         for k, v in arrays.items()}
    t["y"] = nc.dram_tensor("y_out_d", (NP, D), F32, kind="ExternalOutput").ap()
    build(nc, t)
    r = run_bass_kernel_spmd(nc, [arrays], core_ids=[0])
    return r.results[0]["y_out_d"][:N_NODES]
```

```python
from contextlib import ExitStack

import numpy as np

import concourse.bass as bass
import concourse.mybir as mybir

ALU = mybir.AluOpType
ACT = mybir.ActivationFunctionType
AX = mybir.AxisListType
F32 = mybir.dt.float32
I32 = mybir.dt.int32

P = 128
N_NODES, N_EDGES = 6250, 200000
D, EF, GF, HID0, HID1 = 256, 96, 64, 1024, 512
BLOCKS = -(-N_NODES // P)
NP = BLOCKS * P
COLS = 4
GROUP = P * COLS
GROUPS = 8
STEP = GROUP * GROUPS
STEPS = BLOCKS
EP = STEPS * STEP
TILES = GROUPS * COLS
PAD_DEG = (EP - N_EDGES) // (NP - N_NODES)
WIN = 32
WIDE = 160
CHUNK = 8
FULL = 7
SLOTS = (FULL + 1) * CHUNK
SPLIT = 448
ROWS_CHECK = 112
COLS_CHECK = EP // ROWS_CHECK
FINE_RING = 8
SKIP = float(1 << 20)
BIG = 3.4028234663852886e38
LN_EPS = 1e-5
KC = D // P
HC0 = HID0 // P
HC1 = HID1 // P
assert SPLIT * SPLIT == EP and EP - N_EDGES == PAD_DEG * (NP - N_NODES) and STEPS % 2 == 1


class Step:

    def __init__(self, i, par, uses):
        self.i, self.par, self.uses = i, par, uses

    def next(self):
        return Step(self.i + 1, 1 - self.par, self.uses + self.par)

    def before(self):
        return Step(self.i - 1, 1 - self.par, self.uses - (1 - self.par))

    def first(self):
        return isinstance(self.i, int) and self.i == 0

    def last(self):
        return isinstance(self.i, int) and self.i == STEPS - 1


def at(n):
    return Step(n, n % 2, n // 2)


def wait(eng, sem, value):
    if isinstance(value, int) and value <= 0:
        return
    eng.wait_ge(sem, value)


def pipelined(eng, step, last):
    for n in range(4):
        step(at(n), at(n - 2) if n >= 2 else None)
    with eng.Fori(2, STEPS // 2) as it:
        step(Step(it * 2, 0, it), Step(it * 2 - 2, 0, it - 1))
        step(Step(it * 2 + 1, 1, it), Step(it * 2 - 1, 1, it - 1))
    step(at(STEPS - 1), at(STEPS - 3))
    last(at(STEPS - 2))
    last(at(STEPS - 1))


def over_blocks(eng, one):
    one(at(0))
    with eng.Fori(1, BLOCKS // 2 + 1) as it:
        one(Step(it * 2 - 1, 1, it - 1))
        one(Step(it * 2, 0, it))


def build(nc, t):
    ctx = ExitStack()

    def sb(name, shape, dt=F32):
        return ctx.enter_context(nc.sbuf_tensor(name, shape, dt))

    def bank(name):
        return ctx.enter_context(nc.psum_tensor(name, [P, 512], F32))

    def sem(name):
        return ctx.enter_context(nc.semaphore(name))

    with ctx:
        dst_rows_d = nc.dram_tensor("dst_rows_d", [SPLIT, SPLIT], F32).ap()
        x1_d = nc.dram_tensor("x1_d", [NP, D], F32).ap()

        w0x = sb("w0x", [P, KC, HID0])
        w0e = sb("w0e", [EF, 3, HID0])
        w0b = sb("w0b", [P, HC0, D])
        b2_0 = sb("b2_0", [P, D])
        bias0 = sb("bias0", [P, HC0])
        ident = sb("ident", [P, P])
        ones = sb("ones", [P, P])
        iota_f = sb("iota_f", [P, WIDE])
        eps_col = sb("eps_col", [P, 1])
        epsilon = sb("epsilon", [P, 1])
        start = sb("start", [P, BLOCKS + 1])
        idx_f = sb("idx_f", [P, BLOCKS, FULL + 1])
        full_cap = sb("full_cap", [P, BLOCKS, FULL])
        tail_cap = sb("tail_cap", [P, BLOCKS, CHUNK])
        rinv = sb("rinv", [P, BLOCKS])
        has = sb("has", [P, BLOCKS])
        wide_base = sb("wide_base", [1, STEPS], I32)
        place = sb("place", [P, STEPS * 2])
        base_f = sb("base_f", [P, STEPS * GROUPS])
        flag = sb("flag", [1, 1], I32)
        out1T = sb("out1T", [EF, NP])
        aggT = sb("aggT", [P, KC, NP])
        onehot = [sb(f"onehot{j}", [P, TILES, WIN]) for j in range(2)]
        select = [sb(f"select{j}", [P, 2, WIDE]) for j in range(2)]
        dst_t = [sb(f"dst_t{j}", [P, TILES], I32) for j in range(2)]
        w_t = [sb(f"w_t{j}", [P, TILES]) for j in range(2)]
        src_t = [sb(f"src_t{j}", [P, TILES], I32) for j in range(2)]
        dloc = sb("dloc", [P, TILES])
        hT = sb("hT", [P, HC0, P])
        xT_b = [sb(f"xT_b{j}", [P, KC, P]) for j in range(2)]
        xn_b = [sb(f"xn_b{j}", [P, D]) for j in range(2)]
        out_b = [sb(f"out_b{j}", [P, D]) for j in range(2)]
        z1 = sb("z1", [P, HID1])
        x2b = sb("x2b", [P, D])
        o1b = sb("o1b", [EF, P])
        o2b = sb("o2b", [EF, P])
        o3b = sb("o3b", [EF, P])
        rdiag = sb("rdiag", [P, P])
        chunk_max = sb("chunk_max", [P, FULL + 1, EF])
        max_w = sb("max_w", [P, EF])
        max_n = [sb(f"max_n{j}", [P, EF]) for j in range(2)]
        stats = sb("stats", [P, 6])
        mv = sb("mv", [P, 2])
        std = sb("std", [P, 1])
        rstd = sb("rstd", [P, 1])
        ell_idx = [sb(f"ell_idx{j}", [P, FULL + 1], I32) for j in range(2)]
        bad = sb("bad", [P, 5])
        bad_sum = sb("bad_sum", [P, 1])
        agg_in = sb("agg_in", [P, KC, P])

        ELL = SLOTS * EF
        NAT = TILES // 2 * EF
        ARENA = 2 * ELL + 2 * NAT
        arena = sb("arena", [P, ARENA])
        taken = [0]

        def piece(size, rows=P, dt=F32):
            lo = taken[0]
            taken[0] += -(-size // 8) * 8
            assert taken[0] <= ARENA
            v = arena[0:rows, lo:lo + size]
            return v if dt is F32 else v.bitcast(dt)

        ell = [piece(ELL) for j in range(2)]
        attr = [piece(NAT).rearrange("p (t f) -> p t f", f=EF) for j in range(2)]
        taken[0] = 0
        sums_nat = z1[:, D:D + 2 * EF]
        gath = [piece(COLS * D).rearrange("p (c d) -> p c d", d=D) for g in range(GROUPS)]
        w1T = piece(KC * HID1).rearrange("p (c h) -> p c h", c=KC)
        w2T = piece(HC1 * D).rearrange("p (c d) -> p c d", c=HC1)
        b1_1, g1_1, be1_1 = (piece(HID1) for _ in range(3))
        b2_1, g2_1, be2_1 = (piece(D) for _ in range(3))
        msg_nat = [piece(D) for half in range(2)]
        taken[0] = 0
        keys_i = piece(SPLIT, dt=I32)
        keys_f = piece(SPLIT)
        dn_i = piece(COLS_CHECK + 1, ROWS_CHECK, I32)
        dn_f = piece(COLS_CHECK, ROWS_CHECK)
        disorder = piece(COLS_CHECK, ROWS_CHECK)
        fine = [piece(SPLIT) for j in range(FINE_RING)]
        less = piece(SPLIT)
        w0u = piece(HID0, GF)
        u0 = piece(1, GF)
        b1_0 = piece(HC0)
        node_i = piece(BLOCKS, dt=I32)
        node_f = piece(BLOCKS)
        iota_i = piece(WIDE, dt=I32)
        eights_i = piece(CHUNK, dt=I32)
        eights_f = piece(CHUNK)
        limit_i = piece(BLOCKS - 1, 1, I32)
        limit_f = piece(BLOCKS - 1, 1)
        base_b = piece(STEPS * GROUPS, dt=I32)
        base_i = piece(STEPS * GROUPS, 1, I32)
        place_i = piece(STEPS * 2, dt=I32)
        lane = piece(1)
        wide_f = piece(STEPS)
        wide_span = piece(STEPS, 1)
        ends_i = piece(STEPS * GROUPS, 1, I32)
        span_f = piece(STEPS * GROUPS, 1)
        coarse = piece(BLOCKS)
        row_i = piece(BLOCKS, dt=I32)
        in_row = piece(BLOCKS)
        shift = piece(P)
        wrap = piece(P)
        nxt = piece(BLOCKS)
        deg = piece(BLOCKS)
        full_f = piece(BLOCKS * FULL).rearrange("p (b j) -> p b j", j=FULL)
        n_full = piece(BLOCKS)
        tail_at = piece(BLOCKS)
        by_slot = piece(BLOCKS * CHUNK).rearrange("p (b j) -> p b j", j=CHUNK)
        late_f = piece(BLOCKS - 1, 1)
        taken[0] = 0
        out2T = piece(NP, EF)
        cntT = piece(NP, EF)
        g_attr = piece(EF)
        g_attrT = piece(P, EF)
        g_dst = piece(P, 1, I32)
        g_src = piece(1, dt=I32)
        g_w = piece(1)
        g_x = piece(D)
        g_xT = piece(KC * P).rearrange("p (c n) -> p c n", c=KC)
        g_one = piece(1, EF)

        seg = [bank("segA"), bank("segB")]
        hid = [bank("hidA"), bank("hidB")]
        zb = bank("zb")
        maxb = bank("maxb")
        x1b = bank("x1b")
        misc = bank("misc")

        keys_in, dn_in, win_in, u_in = sem("keys_in"), sem("dn_in"), sem("win_in"), sem("u_in")
        w0_in, eps_in, rows_out = sem("w0_in"), sem("eps_in"), sem("rows_out")
        fine_in = [sem(f"fine_in{j}") for j in range(FINE_RING)]
        dst_in = [sem(f"dst_in{j}") for j in range(2)]
        attr_in = [sem(f"attr_in{j}") for j in range(2)]
        ell_in = [sem(f"ell_in{j}") for j in range(2)]
        x_in = [sem(f"x_in{j}") for j in range(2)]
        x1_out = [sem(f"x1_out{j}") for j in range(2)]
        w1_in = sem("w1_in")
        edge_in = [sem(f"edge_in{j}") for j in range(2)]
        gath_in = [sem(f"gath_in{g}") for g in range(GROUPS)]
        x1_in = [sem(f"x1_in{j}") for j in range(2)]
        y_out = [sem(f"y_out{j}") for j in range(2)]
        consts_ready, dn_ready, count_ready = sem("consts_ready"), sem("dn_ready"), sem("count_ready")
        fine_used, start_ready, nxt_ps = sem("fine_used"), sem("start_ready"), sem("nxt_ps")
        bias_ps, bias_ready, bad_ready = sem("bias_ps"), sem("bias_ready"), sem("bad_ready")
        bad_ps, setup_done, ident_zero = sem("bad_ps"), sem("setup_done"), sem("ident_zero")
        ell_clear = sem("ell_clear")
        onehot_ready, seg_ps, seg_added = sem("onehot_ready"), sem("seg_ps"), sem("seg_added")
        dst_float, dst_local, select_ready = sem("dst_float"), sem("dst_local"), sem("select_ready")
        dist_ready, dist_squared = sem("dist_ready"), sem("dist_squared")
        sums_copied, sumsT_ps = sem("sums_copied"), sem("sumsT_ps")
        ell_idx_ready, ell_used, max_ready = sem("ell_idx_ready"), sem("ell_used"), sem("max_ready")
        maxT_ps, rinv_ps, hid_ps, z_ps, x1T_ps = (
            sem("maxT_ps"), sem("rinv_ps"), sem("hid_ps"), sem("z_ps"), sem("x1T_ps"))
        rdiag_ready, o1_ready, o2_ready, relu_ready, std_ready, agg_init = (
            sem("rdiag_ready"), sem("o1_ready"), sem("o2_ready"), sem("relu_ready"),
            sem("std_ready"), sem("agg_init"))
        mean_ready, var_ready, x1_ready = sem("mean_ready"), sem("var_ready"), sem("x1_ready")
        wonehot_ready, msg_ps, msg_added = sem("wonehot_ready"), sem("msg_ps"), sem("msg_added")
        select1_ready, msg_copied, msgT_ps = sem("select1_ready"), sem("msg_copied"), sem("msgT_ps")
        agg_ready, h1_ps, h1_ready, h1T_ps, h1T_ready, h2_ps = (
            sem("agg_ready"), sem("h1_ps"), sem("h1_ready"), sem("h1T_ps"), sem("h1T_ready"),
            sem("h2_ps"))
        var1_ready, std1_ready, y_ready = sem("var1_ready"), sem("std1_ready"), sem("y_ready")
        g_attr_in, g_dst_in, g_src_in, g_w_in, g_gath_in = (
            sem("g_attr_in"), sem("g_dst_in"), sem("g_src_in"), sem("g_w_in"), sem("g_gath_in"))
        g_turned, g_scaled, g_done, g_sums = (
            sem("g_turned"), sem("g_scaled"), sem("g_done"), sem("g_sums"))

        GT = EP // P
        block = ctx.enter_context(nc.Block())

        def is_fast(eng):
            eng.wait_ge(setup_done, 1)
            return eng.value_load(flag[0:1, 0:1], min_val=0, max_val=1) < 1

        @block.sync
        def _(sp):
            sp.dma_start(keys_i, t["keys"].partition_broadcast(P)).then_inc(keys_in, 16)
            sp.dma_start(dn_i, t["dst_rows"]).then_inc(dn_in, 16)
            sp.dma_start(base_b, t["base"].partition_broadcast(P)).then_inc(win_in, 16)
            sp.dma_start(base_i, t["base"].unsqueeze(0)).then_inc(win_in, 16)
            sp.dma_start(ends_i, t["ends"].unsqueeze(0)).then_inc(win_in, 16)
            sp.dma_start(place_i, t["place"]).then_inc(win_in, 16)
            sp.dma_start(lane, t["lane"]).then_inc(win_in, 16)
            sp.dma_start(w0u, t["W1"][D + 3 * EF:, :]).then_inc(u_in, 16)
            sp.dma_start(u0, t["u0"]).then_inc(u_in, 16)
            sp.dma_start(b1_0, t["b1_0"]).then_inc(u_in, 16)
            sp.dma_start(epsilon[:, :], t["epsilon"].to_broadcast([P, 1])).then_inc(eps_in, 16)
            sp.wait_ge(dn_ready, 1)
            sp.dma_start(dst_rows_d.rearrange("a b -> (a b)").rearrange("(p c) -> p c", c=COLS_CHECK),
                         dn_f).then_inc(rows_out, 16)
            sp.dma_start(w0x[:, :, :], t["W1"][0:D, :].rearrange("(c p) h -> p c h", p=P)).then_inc(w0_in, 16)
            sp.dma_start(w0e[:, :, :], t["W1"][D:D + 3 * EF, :].rearrange("(c p) h -> p c h", p=EF)).then_inc(w0_in, 16)
            sp.dma_start(w0b[:, :, :], t["W2"].rearrange("(c p) d -> p c d", p=P)).then_inc(w0_in, 16)
            sp.dma_start(b2_0[:, :], t["b2_0"].partition_broadcast(P)).then_inc(w0_in, 16)

            def load_x(m):
                wait(sp, z_ps, m.i - 1)
                wait(sp, var_ready, m.i - 1)
                sp.dma_start(xT_b[m.par][:, :, :], t["xT"].rearrange("(c p) n -> p c n", p=P)
                             [:, :, bass.ds(m.i * P, P)]).then_inc(x_in[m.par], 16)
                sp.dma_start(xn_b[m.par][:, :], t["x"][bass.ds(m.i * P, P), :]).then_inc(x_in[m.par], 16)

            def phase1(s, m):
                wait(sp, dist_ready, s.i - 1)
                sp.dma_start(dst_t[s.par][:, :], t["dst_s"][bass.ds(s.i, 1), :, :]
                             .rearrange("a p t -> (a p) t")).then_inc(dst_in[s.par], 16)
                for half in range(2):
                    wait(sp, seg_ps, s.i * 2 - 1 + half)
                    rows = t["attr"].rearrange("(s g p c) f -> s p g (c f)", g=GROUPS, p=P, c=COLS)
                    sp.dma_start(attr[half].rearrange("p (g c) f -> p g (c f)", c=COLS),
                                 rows[bass.ds(s.i, 1), :, half * 4:half * 4 + 4, :]
                                 .rearrange("a p g r -> (a p) g r")).then_inc(attr_in[half], 16)
                if m is not None:
                    load_x(m)

            def load_second_layer():
                for out, name in ((w1T, "w1T"), (w2T, "w2T")):
                    sp.dma_start(out, t[name].rearrange("(c p) n -> p c n", p=P)).then_inc(w1_in, 16)
                for out, name in ((b1_1, "b1_1"), (g1_1, "g1_1"), (be1_1, "be1_1"),
                                  (b2_1, "b2_1"), (g2_1, "g2_1"), (be2_1, "be2_1")):
                    sp.dma_start(out, t[name].partition_broadcast(P)).then_inc(w1_in, 16)

            def all_x1(eng):
                for j in range(2):
                    eng.wait_ge(x1_out[j], 16 * ((BLOCKS + 1 - j) // 2))

            def load_x1(m):
                wait(sp, y_ready, m.i - 1)
                sp.dma_start(xn_b[m.par][:, :], x1_d[bass.ds(m.i * P, P), :]).then_inc(x1_in[m.par], 16)

            def phase2(s, m):
                wait(sp, msg_ps, (s.i - 1) * GROUPS)
                wait(sp, wonehot_ready, s.i - 1)
                for out, name in ((src_t, "src_s"), (dst_t, "dst_s"), (w_t, "w_s")):
                    sp.dma_start(out[s.par][:, :], t[name][bass.ds(s.i, 1), :, :]
                                 .rearrange("a p t -> (a p) t")).then_inc(edge_in[s.par], 16)
                if m is not None:
                    load_x1(m)
                elif s.i == 1:
                    sp.wait_ge(var_ready, BLOCKS)
                    all_x1(sp)

            with sp.If(is_fast(sp)):
                pipelined(sp, phase1, load_x)
                sp.wait_ge(ell_used, STEPS)
                sp.wait_ge(seg_ps, 2 * STEPS)
                load_second_layer()
                pipelined(sp, phase2, load_x1)
            with sp.Else():
                with sp.Fori(0, GT) as k:
                    sp.wait_ge(g_done, k)
                    sp.dma_start(g_attr, t["attr"][bass.ds(k * P, P), :]).then_inc(g_attr_in, 16)
                    sp.dma_start(g_dst, t["dst_f"][bass.ds(k, 1), :]).then_inc(g_dst_in, 16)
                over_blocks(sp, load_x)
                all_x1(sp)
                with sp.Fori(0, GT) as k:
                    sp.wait_ge(g_done, k + GT)
                    sp.dma_start(g_src, t["src_f"][bass.ds(k * P, P), :]).then_inc(g_src_in, 16)
                    sp.dma_start(g_w, t["w_f"][bass.ds(k * P, P), :]).then_inc(g_w_in, 16)
                    sp.dma_start(g_dst, t["dst_f"][bass.ds(k, 1), :]).then_inc(g_dst_in, 16)
                sp.wait_ge(g_done, 2 * GT)
                load_second_layer()
                over_blocks(sp, load_x1)

        @block.gpsimd
        def _(pool):
            pool.iota(node_i, pattern=[[P, BLOCKS]], base=0, channel_multiplier=1).then_inc(consts_ready, 1)
            pool.iota(iota_i, pattern=[[1, WIDE]], base=0, channel_multiplier=0).then_inc(consts_ready, 1)
            pool.iota(eights_i, pattern=[[CHUNK, CHUNK]], base=0, channel_multiplier=0).then_inc(consts_ready, 1)
            pool.iota(limit_i, pattern=[[STEP, BLOCKS - 1]], base=2 * STEP, channel_multiplier=0).then_inc(consts_ready, 1)
            pool.memset(ident[:, :], 0.0).then_inc(ident_zero, 1)
            pool.memset(shift, 0.0).then_inc(ident_zero, 1)
            pool.memset(wrap, 0.0).then_inc(ident_zero, 1)
            pool.wait_ge(ident_zero, 3)
            pool.affine_select(out=ident[:, :], in_=ident[:, :], compare_op=ALU.not_equal, fill=1.0,
                               base=0, pattern=[[-1, P]], channel_multiplier=1).then_inc(consts_ready, 1)
            pool.affine_select(out=shift, in_=shift, compare_op=ALU.not_equal, fill=1.0,
                               base=-1, pattern=[[-1, P]], channel_multiplier=1).then_inc(consts_ready, 1)
            pool.memset(wrap[0:1, P - 1:P], 1.0).then_inc(consts_ready, 1)
            pool.memset(ones[:, :], 1.0).then_inc(consts_ready, 1)
            pool.memset(eps_col[:, :], LN_EPS).then_inc(consts_ready, 1)
            pool.wait_ge(rows_out, 16)
            for b in range(BLOCKS):
                pool.wait_ge(count_ready, b + 1)
                if b >= FINE_RING:
                    pool.wait_ge(fine_used, b - FINE_RING + 1)
                pool.indirect_dma_start(fine[b % FINE_RING], None, dst_rows_d,
                                        bass.IndirectOffsetOnAxis(ap=row_i[:, b:b + 1], axis=0),
                                        bounds_check=SPLIT - 1, oob_is_err=False
                                        ).then_inc(fine_in[b % FINE_RING], 16)

            bound = pool.alloc_register("bound")

            def wait_for_bound(sem_, value, last_row):
                wait(pool, sem_, value)
                pool.reg_alu(bound, bound, last_row, ALU.min)
                return pool.snap(bound, min_val=0, max_val=last_row)

            def distances(s):
                wait_for_bound(dst_in[s.par], s.uses * 16 + 16, EP - CHUNK)
                pool.tensor_copy(dloc[:, :], dst_t[s.par][:, :]).then_inc(dst_float, 1)
                pool.wait_ge(dst_float, s.i + 1)
                pool.tensor_tensor(dloc[:, :].rearrange("p (g c) -> p g c", c=COLS),
                                   dloc[:, :].rearrange("p (g c) -> p g c", c=COLS),
                                   base_f[:, bass.ds(s.i * GROUPS, GROUPS)].unsqueeze(2)
                                   .to_broadcast([P, GROUPS, COLS]), ALU.subtract).then_inc(dst_local, 1)
                wait_for_bound(dst_local, s.i + 1, EP - CHUNK)
                wait(pool, seg_ps, (s.i - 1) * 2)
                pool.tensor_tensor(onehot[s.par][:, :, :], dloc[:, :].unsqueeze(2).to_broadcast([P, TILES, WIN]),
                                   iota_f[:, 0:WIN].unsqueeze(1).to_broadcast([P, TILES, WIN]),
                                   ALU.subtract).then_inc(dist_ready, 1)
                wait_for_bound(dist_ready, s.i + 1, EP - CHUNK)

            def phase1(s, m):
                wait(pool, ell_used, s.i - 1)
                pool.tensor_copy(ell_idx[s.par][:, :], idx_f[:, bass.ds(s.i, 1), :]
                                 .rearrange("p a j -> p (a j)")).then_inc(ell_idx_ready, 1)
                last_row = wait_for_bound(ell_idx_ready, s.i + 1, EP - CHUNK)
                for j in range(FULL + 1):
                    pool.indirect_dma_start(ell[s.par][:, j * CHUNK * EF:(j + 1) * CHUNK * EF], None,
                                            t["attr"], bass.IndirectOffsetOnAxis(
                                                ap=ell_idx[s.par][:, j:j + 1], axis=0),
                                            bounds_check=last_row, oob_is_err=False
                                            ).then_inc(ell_in[s.par], 16)
                if not s.last():
                    distances(s.next())

            def phase2(s, m):
                pool.wait_ge(edge_in[s.par], s.uses * 48 + 48)
                for g in range(GROUPS):
                    last_row = wait_for_bound(msg_ps, (s.i - 1) * GROUPS + g + 1, NP - 1)
                    for c in range(COLS):
                        pool.indirect_dma_start(gath[g][:, c, :], None, x1_d,
                                                bass.IndirectOffsetOnAxis(
                                                    ap=src_t[s.par][:, g * COLS + c:g * COLS + c + 1], axis=0),
                                                bounds_check=last_row, oob_is_err=False
                                                ).then_inc(gath_in[g], 16)

            def all_x1():
                for j in range(2):
                    pool.wait_ge(x1_out[j], 16 * ((BLOCKS + 1 - j) // 2))

            pool.reg_mov(bound, EP)
            with pool.If(is_fast(pool)):
                for j in range(2):
                    pool.memset(ell[j], 0.0).then_inc(ell_clear, 1)
                pool.wait_ge(ell_clear, 2)
                distances(at(0))
                pipelined(pool, phase1, lambda m: None)
                all_x1()
                pool.wait_ge(ell_used, STEPS)
                pool.wait_ge(seg_ps, 2 * STEPS)
                pipelined(pool, phase2, lambda m: None)
            with pool.Else():
                all_x1()
                with pool.Fori(0, GT) as k:
                    last_row = wait_for_bound(g_src_in, k * 16 + 16, NP - 1)
                    pool.indirect_dma_start(g_x, None, x1_d, bass.IndirectOffsetOnAxis(ap=g_src, axis=0),
                                            bounds_check=last_row, oob_is_err=False).then_inc(g_gath_in, 16)
                    pool.wait_ge(g_gath_in, k * 16 + 16)

        @block.tensor
        def _(pe):
            pe.wait_ge(consts_ready, 9)
            pe.wait_ge(u_in, 48)
            for c in range(HC0):
                mm = pe.matmul(misc[:, c:c + 1], w0u[:, c * P:(c + 1) * P], u0, start=True, stop=True)
            mm.then_inc(bias_ps, 1)
            pe.wait_ge(start_ready, 1)
            pe.matmul(zb[:, 0:BLOCKS], shift, start[:, 0:BLOCKS], start=True, stop=False)
            pe.matmul(zb[:, 0:BLOCKS], wrap, start[:, 1:BLOCKS + 1], start=False, stop=True).then_inc(nxt_ps, 1)
            pe.wait_ge(bad_ready, 1)
            pe.matmul(maxb[0:1, 0:1], bad_sum[:, :], ones[:, 0:1], start=True, stop=True).then_inc(bad_ps, 1)
            pe.wait_ge(w0_in, 64)

            def sums(s):
                pe.wait_ge(onehot_ready, s.i + 1)
                wait(pe, sums_copied, s.i)
                for half in range(2):
                    pe.wait_ge(attr_in[half], s.i * 16 + 16)
                    for g in range(GROUPS // 2):
                        for c in range(COLS):
                            mm = pe.matmul(seg[0][g * WIN:(g + 1) * WIN, half * EF:(half + 1) * EF],
                                           onehot[s.par][:, half * 16 + g * COLS + c, :],
                                           attr[half][:, g * COLS + c, :],
                                           start=(c == 0), stop=(c == COLS - 1))
                    mm.then_inc(seg_ps, 1)

            def turn_sums(s):
                pe.wait_ge(select_ready, s.i + 1)
                pe.wait_ge(sums_copied, s.i + 1)
                wait(pe, seg_added, s.i)
                for half in range(2):
                    mm = pe.matmul(seg[1][0:EF, 0:WIDE], sums_nat[:, half * EF:(half + 1) * EF],
                                   select[s.par][:, half, :], start=(half == 0), stop=(half == 1))
                mm.then_inc(sumsT_ps, 1)

            def hidden(m, parts, first, last):
                for half in range(2):
                    for c in range(HC0 // 2):
                        h = half * (HC0 // 2) + c
                        for n, (w, x) in enumerate(parts):
                            mm = pe.matmul(hid[half][:, c * P:(c + 1) * P], w[:, h * P:(h + 1) * P], x,
                                           start=(first and c == 0 and n == 0),
                                           stop=(last and n == len(parts) - 1), skip_group_check=True)
                    if last:
                        mm.then_inc(hid_ps, 1)

            def turn_x1(m):
                pe.wait_ge(x1_ready, m.i + 1)
                wait(pe, agg_init, m.i)
                for c in range(KC):
                    mm = pe.transpose(x1b[:, c * P:(c + 1) * P], out_b[m.par][:, c * P:(c + 1) * P], ident[:, :])
                mm.then_inc(x1T_ps, 1)

            def turn_max(m):
                pe.wait_ge(max_ready, m.i + 1)
                wait(pe, o2_ready, m.i)
                pe.transpose(maxb[0:EF, 0:P], max_n[m.par][:, :], ident[:, :]).then_inc(maxT_ps, 1)

            def spread_rinv(m):
                pe.wait_ge(rdiag_ready, m.i + 1)
                wait(pe, mean_ready, m.i)
                pe.matmul(misc[0:EF, 0:P], ones[:, 0:EF], rdiag[:, :], start=True, stop=True).then_inc(rinv_ps, 1)

            def hidden_of_x(m):
                wait(pe, relu_ready, m.i * 2)
                pe.wait_ge(x_in[m.par], m.uses * 32 + 32)
                hidden(m, [(w0x[:, k, :], xT_b[m.par][:, k, :]) for k in range(KC)], True, False)
                if not m.first():
                    turn_x1(m.before())

            def hidden_of_edges(m):
                pe.wait_ge(o1_ready, m.i + 1)
                pe.wait_ge(o2_ready, m.i + 1)
                pe.wait_ge(mean_ready, m.i + 1)
                hidden(m, [(w0e[:, 0, :], o1b[:, :]), (w0e[:, 1, :], o2b[:, :]), (w0e[:, 2, :], o3b[:, :])],
                       False, True)

            def second(m):
                wait(pe, var_ready, m.i)
                for c in range(HC0):
                    if c % (HC0 // 2) == 0:
                        pe.wait_ge(relu_ready, m.i * 2 + 1 + c // (HC0 // 2))
                    mm = pe.matmul(zb[:, 0:D], hT[:, c, :], w0b[:, c, :], start=(c == 0), stop=(c == HC0 - 1))
                mm.then_inc(z_ps, 1)

            def mlp0(m):
                hidden_of_x(m)
                hidden_of_edges(m)
                second(m)

            def phase1(s, m):
                if m is not None:
                    turn_max(m)
                    spread_rinv(m)
                sums(s)
                if m is not None:
                    hidden_of_x(m)
                turn_sums(s)
                if m is not None:
                    hidden_of_edges(m)
                    second(m)

            def last1(m):
                turn_max(m)
                spread_rinv(m)
                mlp0(m)

            def messages(s, g):
                half, q = g // 4, g % 4
                if q == 0:
                    wait(pe, msg_copied, s.i * 2 - 1 + half)
                pe.wait_ge(gath_in[g], s.i * 16 * COLS + 16 * COLS)
                for c in range(COLS):
                    mm = pe.matmul(seg[half][q * WIN:(q + 1) * WIN, 0:D], onehot[s.par][:, g * COLS + c, :],
                                   gath[g][:, c, :], start=(c == 0), stop=(c == COLS - 1))
                mm.then_inc(msg_ps, 1)

            def turn_messages(s):
                pe.wait_ge(select1_ready, s.i + 1)
                pe.wait_ge(msg_copied, s.i * 2 + 2)
                wait(pe, msg_added, s.i)
                for k in range(KC):
                    for half in range(2):
                        mm = pe.matmul(x1b[:, k * WIDE:(k + 1) * WIDE], msg_nat[half][:, k * P:(k + 1) * P],
                                       select[s.par][:, half, :], start=(half == 0), stop=(half == 1))
                mm.then_inc(msgT_ps, 1)

            def first1(m):
                pe.wait_ge(agg_ready, m.i + 1)
                wait(pe, var1_ready, m.i * 3 - 2)
                for k in range(KC):
                    mm = pe.matmul(hid[0][:, :], agg_in[:, k, :], w1T[:, k, :], start=(k == 0), stop=(k == KC - 1))
                mm.then_inc(h1_ps, 1)

            def turn_h1(m):
                pe.wait_ge(h1_ready, m.i + 1)
                wait(pe, h1T_ready, m.i)
                for c in range(HC1):
                    mm = pe.transpose(hid[1][:, c * P:(c + 1) * P], z1[:, c * P:(c + 1) * P], ident[:, :])
                mm.then_inc(h1T_ps, 1)

            def second1(m):
                pe.wait_ge(h1T_ready, m.i + 1)
                wait(pe, var1_ready, m.i * 3 - 1)
                for c in range(HC1):
                    mm = pe.matmul(zb[:, 0:D], hT[:, c, :], w2T[:, c, :], start=(c == 0), stop=(c == HC1 - 1))
                mm.then_inc(h2_ps, 1)

            def mlp1(m):
                first1(m)
                turn_h1(m)
                second1(m)

            def phase2(s, m):
                pe.wait_ge(wonehot_ready, s.i + 1)
                for g in range(GROUPS):
                    messages(s, g)
                    if g == 1 and m is not None:
                        first1(m)
                    if g == 3 and m is not None:
                        turn_h1(m)
                    if g == 5 and m is not None:
                        second1(m)
                turn_messages(s)

            with pe.If(is_fast(pe)):
                pipelined(pe, phase1, last1)
                turn_x1(at(BLOCKS - 1))
                pe.wait_ge(agg_init, BLOCKS)
                pe.wait_ge(w1_in, 16 * 8)
                pipelined(pe, phase2, mlp1)
            with pe.Else():
                with pe.Fori(0, GT) as k:
                    pe.wait_ge(g_attr_in, k * 16 + 16)
                    pe.transpose(misc[0:EF, 0:P], g_attr, ident[:, :]).then_inc(g_turned, 1)
                over_blocks(pe, mlp0)
                turn_x1(at(BLOCKS - 1))
                with pe.Fori(0, GT) as k:
                    pe.wait_ge(g_scaled, k + 1)
                    for c in range(KC):
                        mm = pe.transpose(misc[:, c * P:(c + 1) * P], g_x[:, c * P:(c + 1) * P], ident[:, :])
                    mm.then_inc(g_turned, 1)
                pe.wait_ge(w1_in, 16 * 8)
                over_blocks(pe, mlp1)

        @block.scalar
        def _(act):
            def turned_x1(m):
                act.wait_ge(x1T_ps, m.i + 1)
                act.activation(aggT[:, :, bass.ds(m.i * P, P)], x1b[:, 0:D].rearrange("p (c n) -> p c n", c=KC),
                               ACT.Copy, scale=epsilon[:, 0:1]).then_inc(agg_init, 1)

            def deviation(m, have, want, n=0, per=1):
                act.wait_ge(have, m.i * per + n + 1)
                act.activation(std[:, :], mv[:, 1:2], ACT.Sqrt, bias=eps_col[:, 0:1]).then_inc(want, 1)

            def diagonal(m):
                wait(act, rinv_ps, m.i)
                act.activation(rdiag[:, :], ident[:, :], ACT.Copy,
                               scale=rinv[:, bass.ds(m.i, 1)]).then_inc(rdiag_ready, 1)

            def sums_in(m, fast):
                if fast:
                    act.wait_ge(seg_added, STEPS if m.last() else m.i + 2)
                wait(act, hid_ps, m.i * 2)
                wait(act, mean_ready, m.i)
                act.activation(o1b[:, :], out1T[:, bass.ds(m.i * P, P)], ACT.Copy).then_inc(o1_ready, 1)

            def maxima_in(m, fast):
                wait(act, hid_ps, m.i * 2)
                if fast:
                    act.wait_ge(maxT_ps, m.i + 1)
                    act.activation(o2b[:, :], maxb[0:EF, 0:P], ACT.Copy).then_inc(o2_ready, 1)
                else:
                    act.activation(o2b[:, :], out2T[:, bass.ds(m.i * P, P)], ACT.Copy).then_inc(o2_ready, 1)

            def copy_sums(s):
                act.wait_ge(seg_ps, s.i * 2 + 2)
                wait(act, sumsT_ps, s.i)
                act.activation(sums_nat, seg[0][:, 0:2 * EF], ACT.Copy).then_inc(sums_copied, 1)

            def mlp0(m, fast):
                if not m.first():
                    turned_x1(m.before())
                wait(act, z_ps, m.i)
                for c in range(HC0):
                    half, q = c // (HC0 // 2), c % (HC0 // 2)
                    if q == 0:
                        act.wait_ge(hid_ps, m.i * 2 + 1 + half)
                    relu = act.activation(hT[:, c, :], hid[half][:, q * P:(q + 1) * P], ACT.Relu,
                                          bias=bias0[:, c:c + 1])
                    if q == HC0 // 2 - 1:
                        relu.then_inc(relu_ready, 1)
                if fast and not m.last():
                    diagonal(m.next())
                    sums_in(m.next(), True)
                deviation(m, var_ready, std_ready)
                act.wait_ge(x1_ready, m.i + 1)
                act.dma_start(x1_d[bass.ds(m.i * P, P), :], out_b[m.par][:, :]).then_inc(x1_out[m.par], 16)

            def window_matrix(s):
                act.wait_ge(dist_ready, s.i + 1)
                act.activation(onehot[s.par][:, :, :], onehot[s.par][:, :, :], ACT.Square
                               ).then_inc(dist_squared, 1)
                act.wait_ge(dist_squared, s.i + 1)
                act.activation(onehot[s.par][:, :, :], onehot[s.par][:, :, :], ACT.Relu,
                               bias=ones[:, 0:1], scale=-1.0).then_inc(onehot_ready, 1)

            def phase1(s, m):
                if m is not None:
                    maxima_in(m, True)
                copy_sums(s)
                if not s.last():
                    window_matrix(s.next())
                if m is None and s.i == 1:
                    sums_in(at(0), True)
                if m is not None:
                    mlp0(m, True)

            def block0(m, fast):
                if not fast:
                    sums_in(m, False)
                maxima_in(m, fast)
                mlp0(m, fast)

            def copy_messages(s, half):
                act.wait_ge(msg_ps, s.i * GROUPS + half * 4 + 4)
                wait(act, msgT_ps, s.i)
                act.activation(msg_nat[half], seg[half][:, 0:D], ACT.Copy).then_inc(msg_copied, 1)

            def first1(m, fast):
                if fast:
                    act.wait_ge(msg_added, STEPS if m.last() else m.i + 2)
                wait(act, h1_ps, m.i)
                act.activation(agg_in[:, :, :], aggT[:, :, bass.ds(m.i * P, P)], ACT.Copy).then_inc(agg_ready, 1)
                deviation(m, var1_ready, std1_ready, 0, 3)

            def second1(m):
                act.wait_ge(h1T_ps, m.i + 1)
                wait(act, h2_ps, m.i)
                act.activation(hT[:, 0:HC1, :], hid[1][:, :].rearrange("p (c n) -> p c n", c=HC1),
                               ACT.Relu).then_inc(h1T_ready, 1)
                deviation(m, var1_ready, std1_ready, 1, 3)
                deviation(m, var1_ready, std1_ready, 2, 3)
                act.wait_ge(y_ready, m.i + 1)
                act.dma_start(t["y"][bass.ds(m.i * P, P), :], out_b[m.par][:, :]).then_inc(y_out[m.par], 16)

            def mlp1(m, fast):
                first1(m, fast)
                second1(m)

            def phase2(s, m):
                if m is not None:
                    first1(m, True)
                copy_messages(s, 0)
                if m is not None:
                    second1(m)
                copy_messages(s, 1)

            act.wait_ge(eps_in, 16)
            with act.If(is_fast(act)):
                diagonal(at(0))
                window_matrix(at(0))
                pipelined(act, phase1, lambda m: block0(m, True))
                turned_x1(at(BLOCKS - 1))
                pipelined(act, phase2, lambda m: mlp1(m, True))
            with act.Else():
                act.wait_ge(g_sums, 1)
                over_blocks(act, lambda m: block0(m, False))
                turned_x1(at(BLOCKS - 1))
                act.wait_ge(g_done, 2 * GT)
                over_blocks(act, lambda m: mlp1(m, False))
            for j in range(2):
                act.wait_ge(y_out[j], 16 * ((BLOCKS + 1 - j) // 2))

        @block.vector
        def _(dve):
            tt, ts, red = dve.tensor_tensor, dve.tensor_scalar, dve.tensor_reduce

            def settle():
                dve.drain()

            dve.memset(start[:, BLOCKS:BLOCKS + 1], float(EP))
            dve.memset(bad[:, :], 0.0)
            dve.memset(out1T[:, :], 0.0)
            dve.wait_ge(dn_in, 16)
            dve.tensor_copy(dn_f, dn_i[:, 0:COLS_CHECK]).then_inc(dn_ready, 1)
            dve.wait_ge(keys_in, 16)
            dve.tensor_copy(keys_f, keys_i)
            dve.wait_ge(consts_ready, 9)
            dve.tensor_copy(node_f, node_i)
            settle()
            lag = FINE_RING - 2
            for b in range(BLOCKS + lag):
                if b < BLOCKS:
                    ts(less, keys_f, node_f[:, b:b + 1], None, ALU.is_lt, ALU.add, accum_out=coarse[:, b:b + 1])
                    settle()
                    ts(row_i[:, b:b + 1], coarse[:, b:b + 1], -1.0, 0.0, ALU.add, ALU.max).then_inc(count_ready, 1)
                if b >= lag:
                    d = b - lag
                    dve.wait_ge(fine_in[d % FINE_RING], 16 * (d // FINE_RING + 1))
                    ts(less, fine[d % FINE_RING], node_f[:, d:d + 1], None, ALU.is_lt, ALU.add,
                       accum_out=in_row[:, d:d + 1]).then_inc(fine_used, 1)
                    settle()
            ts(coarse, coarse, -1.0, 0.0, ALU.add, ALU.max)
            settle()
            dve.scalar_tensor_tensor(out=start[:, 0:BLOCKS], in0=coarse, scalar=float(SPLIT), in1=in_row,
                                     op0=ALU.mult, op1=ALU.add).then_inc(start_ready, 1)

            tt(disorder, dn_i[:, 0:COLS_CHECK], dn_i[:, 1:COLS_CHECK + 1], ALU.is_gt)
            dve.wait_ge(win_in, 80)
            tt(span_f, ends_i, base_i, ALU.subtract)
            ts(wide_f, base_b.rearrange("p (s g) -> p g s", g=GROUPS)[:, 0, :], float(NP - WIDE), None, ALU.min)
            ts(place[:, :], place_i, lane, None, ALU.add)
            dve.tensor_copy(base_f[:, :], base_b)
            dve.tensor_copy(iota_f[:, :], iota_i)
            dve.tensor_copy(eights_f, eights_i)
            dve.tensor_copy(limit_f, limit_i)
            settle()
            tt(wide_span, ends_i.rearrange("p (s g) -> p g s", g=GROUPS)[:, GROUPS - 1, :], wide_f[0:1, :],
               ALU.subtract)
            dve.tensor_copy(wide_base[:, :], wide_f[0:1, :])
            tt(place[:, :].rearrange("p (s h) -> p s h", h=2), place[:, :].rearrange("p (s h) -> p s h", h=2),
               wide_f.unsqueeze(2).to_broadcast([P, STEPS, 2]), ALU.subtract)
            red(bad[0:ROWS_CHECK, 0:1], disorder, AX.X, ALU.add)
            ts(span_f, span_f, float(WIN), None, ALU.is_ge)
            settle()
            ts(wide_span, wide_span, float(WIDE), None, ALU.is_ge)
            tt(late_f, start[0:1, 1:BLOCKS], limit_f, ALU.is_gt)
            settle()
            red(bad[0:1, 1:2], span_f, AX.X, ALU.add)
            red(bad[0:1, 2:3], late_f, AX.X, ALU.add)
            red(bad[0:1, 4:5], wide_span, AX.X, ALU.add)

            dve.wait_ge(nxt_ps, 1)
            dve.tensor_copy(nxt, zb[:, 0:BLOCKS])
            settle()
            tt(deg, nxt, start[:, 0:BLOCKS], ALU.subtract)
            settle()
            ts(n_full, deg, float(SLOTS), None, ALU.is_gt)
            tt(full_f, deg.unsqueeze(2).to_broadcast([P, BLOCKS, FULL]),
               eights_f[:, 1:CHUNK].unsqueeze(1).to_broadcast([P, BLOCKS, FULL]), ALU.is_gt)
            ts(rinv[:, :], deg, 1.0, None, ALU.max)
            ts(has[:, :], deg, 1.0, None, ALU.min)
            settle()
            red(bad[:, 3:4], n_full, AX.X, ALU.add)
            dve.reciprocal(rinv[:, :], rinv[:, :])
            ts(full_cap[:, :, :], full_f, 0.5, 2.0, ALU.subtract, ALU.mult)
            settle()
            red(bad_sum[:, :], bad[:, :], AX.X, ALU.add).then_inc(bad_ready, 1)
            red(n_full, full_f, AX.X, ALU.add)
            ts(full_cap[:, :, :], full_cap[:, :, :], BIG, None, ALU.mult)
            tt(idx_f[:, :, 0:FULL], start[:, 0:BLOCKS].unsqueeze(2).to_broadcast([P, BLOCKS, FULL]),
               eights_f[:, 0:FULL].unsqueeze(1).to_broadcast([P, BLOCKS, FULL]), ALU.add)
            settle()
            ts(full_f, full_f, -SKIP, SKIP, ALU.mult, ALU.add)
            settle()
            tt(idx_f[:, :, 0:FULL], idx_f[:, :, 0:FULL], full_f, ALU.add)
            dve.scalar_tensor_tensor(out=tail_at, in0=n_full, scalar=float(CHUNK), in1=start[:, 0:BLOCKS],
                                     op0=ALU.mult, op1=ALU.add)
            settle()
            ts(idx_f[:, :, FULL:FULL + 1], tail_at.unsqueeze(2), float(EP - CHUNK), None, ALU.min)
            settle()
            ts(eights_f, eights_f, 1.0 / CHUNK, None, ALU.mult)
            settle()
            tt(by_slot, idx_f[:, :, FULL:FULL + 1].to_broadcast([P, BLOCKS, CHUNK]),
               eights_f.unsqueeze(1).to_broadcast([P, BLOCKS, CHUNK]), ALU.add)
            settle()
            tt(tail_cap[:, :, :], by_slot, tail_at.unsqueeze(2).to_broadcast([P, BLOCKS, CHUNK]), ALU.is_ge)
            tt(by_slot, by_slot, nxt.unsqueeze(2).to_broadcast([P, BLOCKS, CHUNK]), ALU.is_lt)
            settle()
            tt(tail_cap[:, :, :], tail_cap[:, :, :], by_slot, ALU.mult)
            settle()
            ts(tail_cap[:, :, :], tail_cap[:, :, :], 0.5, 2.0, ALU.subtract, ALU.mult)
            settle()
            ts(tail_cap[:, :, :], tail_cap[:, :, :], BIG, None, ALU.mult)
            dve.wait_ge(bias_ps, 1)
            tt(bias0[:, :], misc[:, 0:HC0], b1_0, ALU.add)
            dve.wait_ge(bad_ps, 1)
            ts(flag[:, :], maxb[0:1, 0:1], 1.0, None, ALU.min)
            settle()
            dve.memset(mv[:, :], 0.0).then_inc(setup_done, 1)

            def window_of(s):
                return dve.value_load(wide_base[0:1, bass.ds(s.i, 1)], min_val=0, max_val=NP - WIDE)

            def selection(s, ready):
                for half in range(2):
                    sel = ts(select[s.par][:, half, :], iota_f[:, :], place[:, bass.ds(s.i * 2 + half, 1)], None,
                             ALU.is_equal)
                sel.then_inc(ready, 1)

            def weighted_matrix(s):
                dve.wait_ge(edge_in[s.par], s.uses * 48 + 48)
                wait(dve, msg_ps, (s.i - 1) * GROUPS)
                tt(dloc[:, :].rearrange("p (g c) -> p g c", c=COLS),
                   dst_t[s.par][:, :].rearrange("p (g c) -> p g c", c=COLS),
                   base_f[:, bass.ds(s.i * GROUPS, GROUPS)].unsqueeze(2).to_broadcast([P, GROUPS, COLS]),
                   ALU.subtract)
                settle()
                tt(onehot[s.par][:, :, :], dloc[:, :].unsqueeze(2).to_broadcast([P, TILES, WIN]),
                   iota_f[:, 0:WIN].unsqueeze(1).to_broadcast([P, TILES, WIN]), ALU.is_equal)
                settle()
                tt(onehot[s.par][:, :, :], onehot[s.par][:, :, :],
                   w_t[s.par][:, :].unsqueeze(2).to_broadcast([P, TILES, WIN]),
                   ALU.mult).then_inc(wonehot_ready, 1)
                settle()

            def add_sums(s):
                to = out1T[:, bass.ds(window_of(s), WIDE)]
                dve.wait_ge(sumsT_ps, s.i + 1)
                tt(to, to, seg[1][0:EF, 0:WIDE], ALU.add).then_inc(seg_added, 1)
                settle()

            def add_messages(s):
                to = aggT[:, :, bass.ds(window_of(s), WIDE)]
                dve.wait_ge(msgT_ps, s.i + 1)
                tt(to, to, x1b[:, 0:KC * WIDE].rearrange("p (c n) -> p c n", c=KC), ALU.add).then_inc(msg_added, 1)
                settle()

            def maxima(s):
                dve.wait_ge(ell_in[s.par], s.uses * 16 * (FULL + 1) + 16 * (FULL + 1))
                tail = ell[s.par][:, FULL * CHUNK * EF:].rearrange("p (k f) -> p k f", f=EF)
                tt(tail, tail, tail_cap[:, bass.ds(s.i, 1), :].rearrange("p a k -> p (a k)")
                   .unsqueeze(2).to_broadcast([P, CHUNK, EF]), ALU.min)
                settle()
                red(chunk_max[:, :, :], ell[s.par].rearrange("p (j k f) -> p j f k", k=CHUNK, f=EF),
                    AX.X, ALU.max).then_inc(ell_used, 1)
                settle()
                tt(chunk_max[:, 0:FULL, :], chunk_max[:, 0:FULL, :],
                   full_cap[:, bass.ds(s.i, 1), :].rearrange("p a j -> p (a j)")
                   .unsqueeze(2).to_broadcast([P, FULL, EF]), ALU.min)
                settle()
                red(max_w[:, :], chunk_max[:, :, :].rearrange("p j f -> p f j"), AX.X, ALU.max)
                settle()
                wait(dve, maxT_ps, s.i - 1)
                ts(max_n[s.par][:, :], max_w[:, :], has[:, bass.ds(s.i, 1)], None, ALU.mult).then_inc(max_ready, 1)

            def mean(m, fast):
                dve.wait_ge(o1_ready, m.i + 1)
                wait(dve, hid_ps, m.i * 2)
                if fast:
                    dve.wait_ge(rinv_ps, m.i + 1)
                    by = misc[0:EF, 0:P]
                else:
                    by = cntT[:, bass.ds(m.i * P, P)]
                tt(o3b[:, :], o1b[:, :], by, ALU.mult).then_inc(mean_ready, 1)

            def moments(v, ready):
                settle()
                dve.bn_stats(stats[:, :], v)
                settle()
                dve.bn_aggr(mv[:, :], stats[:, :]).then_inc(ready, 1)

            def normed(out, v, ready, count):
                dve.wait_ge(ready, count)
                dve.reciprocal(rstd[:, :], std[:, :])
                settle()
                return ts(out, v, mv[:, 0:1], rstd[:, 0:1], ALU.subtract, ALU.mult)

            def norm0(m):
                dve.wait_ge(x_in[m.par], m.uses * 32 + 32)
                dve.scalar_tensor_tensor(out=x2b[:, :], in0=xn_b[m.par][:, :], scalar=2.0, in1=b2_0[:, :],
                                         op0=ALU.mult, op1=ALU.add)
                settle()
                dve.wait_ge(z_ps, m.i + 1)
                tt(z1[:, 0:D], zb[:, 0:D], x2b[:, :], ALU.add)
                moments(z1[:, 0:D], var_ready)
                wait(dve, x1_out[m.par], m.uses * 16)
                wait(dve, x1T_ps, m.i - 1)
                normed(out_b[m.par][:, :], z1[:, 0:D], std_ready, m.i + 1).then_inc(x1_ready, 1)

            def norm_hidden(m):
                dve.wait_ge(h1_ps, m.i + 1)
                wait(dve, h1T_ps, m.i)
                tt(z1[:, :], hid[0][:, :], b1_1, ALU.add)
                moments(z1[:, :], var1_ready)
                normed(z1[:, :], z1[:, :], std1_ready, m.i * 3 + 1)
                settle()
                tt(z1[:, :], z1[:, :], g1_1, ALU.mult)
                settle()
                tt(z1[:, :], z1[:, :], be1_1, ALU.add).then_inc(h1_ready, 1)

            def norm_out(m):
                y = x2b[:, :]
                dve.wait_ge(h2_ps, m.i + 1)
                tt(y, zb[:, 0:D], b2_1, ALU.add)
                moments(y, var1_ready)
                normed(y, y, std1_ready, m.i * 3 + 2)
                settle()
                tt(y, y, g2_1, ALU.mult)
                settle()
                tt(y, y, be2_1, ALU.add)
                settle()
                dve.wait_ge(x1_in[m.par], m.uses * 16 + 16)
                dve.scalar_tensor_tensor(out=y, in0=y, scalar=0.0, in1=xn_b[m.par][:, :],
                                         op0=ALU.max, op1=ALU.add)
                moments(y, var1_ready)
                wait(dve, y_out[m.par], m.uses * 16)
                normed(out_b[m.par][:, :], y, std1_ready, m.i * 3 + 3).then_inc(y_ready, 1)

            def norm1(m):
                norm_hidden(m)
                norm_out(m)

            def phase1(s, m):
                selection(s, select_ready)
                if m is not None:
                    mean(m, True)
                maxima(s)
                add_sums(s)
                if m is not None:
                    norm0(m)

            def last1(m):
                mean(m, True)
                norm0(m)

            def phase2(s, m):
                selection(s, select1_ready)
                if m is not None:
                    norm_hidden(m)
                    norm_out(m)
                if not s.last():
                    weighted_matrix(s.next())
                add_messages(s)

            def edge_by_edge(k, from_ps, to, add):
                dve.wait_ge(g_dst_in, k * 16 + 16)
                dve.tensor_copy(to, from_ps)
                settle()
                with dve.Fori(0, P) as e:
                    node = dve.value_load(g_dst[0:1, bass.ds(e, 1)], min_val=0, max_val=NP - 1)
                    add(node, e)
                    settle()
                dve.memset(rstd[:, :], 0.0).then_inc(g_done, 1)
                settle()

            def sum_and_max(node, e):
                row = g_attrT[:, bass.ds(e, 1)]
                tt(out1T[:, bass.ds(node, 1)], out1T[:, bass.ds(node, 1)], row, ALU.add)
                tt(out2T[:, bass.ds(node, 1)], out2T[:, bass.ds(node, 1)], row, ALU.max)
                tt(cntT[:, bass.ds(node, 1)], cntT[:, bass.ds(node, 1)], g_one, ALU.add)

            def add_message(node, e):
                to = aggT[:, :, bass.ds(node, 1)]
                tt(to, to, g_xT[:, :, bass.ds(e, 1)], ALU.add)

            with dve.If(is_fast(dve)):
                pipelined(dve, phase1, last1)
                weighted_matrix(at(0))
                dve.wait_ge(agg_init, BLOCKS)
                dve.wait_ge(w1_in, 16 * 8)
                pipelined(dve, phase2, norm1)
            with dve.Else():
                dve.memset(out2T, -BIG)
                dve.memset(cntT, 0.0)
                dve.memset(g_one, 1.0)
                settle()
                with dve.Fori(0, GT) as k:
                    dve.wait_ge(g_turned, k + 1)
                    edge_by_edge(k, misc[0:EF, 0:P], g_attrT, sum_and_max)
                ts(g_one, g_one, 1.0, None, ALU.mult)
                settle()
                dve.scalar_tensor_tensor(out=out2T, in0=cntT, scalar=1.0, in1=out2T, op0=ALU.min, op1=ALU.mult)
                settle()
                ts(cntT, cntT, 1.0, None, ALU.max)
                settle()
                dve.reciprocal(cntT, cntT).then_inc(g_sums, 1)
                settle()

                def one(m):
                    mean(m, False)
                    norm0(m)

                over_blocks(dve, one)
                dve.wait_ge(agg_init, BLOCKS)
                with dve.Fori(0, GT) as k:
                    dve.wait_ge(g_gath_in, k * 16 + 16)
                    dve.wait_ge(g_w_in, k * 16 + 16)
                    ts(g_x, g_x, g_w[:, 0:1], None, ALU.mult).then_inc(g_scaled, 1)
                    dve.wait_ge(g_turned, k + GT + 1)
                    edge_by_edge(k + GT, misc[:, 0:D].rearrange("p (c n) -> p c n", c=KC), g_xT, add_message)
                dve.wait_ge(w1_in, 16 * 8)
                over_blocks(dve, norm1)


def kernel(**a):
    from concourse import bacc
    from concourse.bass_utils import run_bass_kernel_spmd

    pad_e, pad_n = EP - N_EDGES, NP - N_NODES
    a = {k: np.asarray(v) for k, v in a.items()}
    pad_dst = np.repeat(np.arange(N_NODES, NP, dtype=np.int32), PAD_DEG)
    src = np.concatenate([a["src"], np.zeros(pad_e, np.int32)])
    dst = np.concatenate([a["dst"], pad_dst])
    weight = np.concatenate([a["edge_weight"], np.zeros(pad_e, np.float32)])
    attr = np.concatenate([a["edge_attr_96"], np.zeros((pad_e, EF), np.float32)])
    x = np.concatenate([a["x"], np.zeros((pad_n, D), np.float32)])

    def by_step(v):
        return v.reshape(STEPS, GROUPS, P, COLS).transpose(0, 2, 1, 3).reshape(STEPS, P, TILES)

    past = np.concatenate([dst, np.full(1, NP, np.int32)])
    arrays = {
        "attr": attr, "x": x, "xT": x.T,
        "src_s": by_step(src), "dst_s": by_step(dst), "w_s": by_step(weight),
        "src_f": src.reshape(EP, 1), "w_f": weight.reshape(EP, 1), "dst_f": dst.reshape(EP // P, P),
        "keys": dst[::SPLIT], "base": dst[::GROUP], "ends": dst[GROUP - 1::GROUP],
        "place": np.repeat(dst[::GROUP].reshape(STEPS * 2, GROUPS // 2).T, WIN, axis=0),
        "lane": np.tile(np.arange(WIN, dtype=np.float32), P // WIN).reshape(P, 1),
        "dst_rows": np.concatenate([dst.reshape(ROWS_CHECK, COLS_CHECK),
                                    past[COLS_CHECK::COLS_CHECK].reshape(ROWS_CHECK, 1)], axis=1),
        "W1": a["L0_gnn_W1"], "W2": a["L0_gnn_W2"], "b1_0": a["L0_gnn_b1"].reshape(HC0, P).T,
        "b2_0": a["L0_gnn_b2"], "u0": a["L0_gnn_u"][0].reshape(GF, 1), "epsilon": a["L1_gnn_epsilon"],
        "w1T": a["L1_gnn_w1"].T, "w2T": a["L1_gnn_w2"].T,
        "b1_1": a["L1_gnn_b1"], "g1_1": a["L1_gnn_g1"], "be1_1": a["L1_gnn_beta1"],
        "b2_1": a["L1_gnn_b2"], "g2_1": a["L1_gnn_g2"], "be2_1": a["L1_gnn_beta2"],
    }
    arrays = {k + "_in": np.ascontiguousarray(v) for k, v in arrays.items()}
    nc = bacc.Bacc("TRN2", target_bir_lowering=False, num_devices=1)
    t = {k[:-3]: nc.dram_tensor(k, v.shape, mybir.dt.from_np(v.dtype), kind="ExternalInput").ap()
         for k, v in arrays.items()}
    t["y"] = nc.dram_tensor("y_out_d", (NP, D), F32, kind="ExternalOutput").ap()
    build(nc, t)
    r = run_bass_kernel_spmd(nc, [arrays], core_ids=[0])
    return r.results[0]["y_out_d"][:N_NODES]
```

```python
from contextlib import ExitStack

import numpy as np

import concourse.bass as bass
import concourse.mybir as mybir

ALU = mybir.AluOpType
ACT = mybir.ActivationFunctionType
AX = mybir.AxisListType
F32 = mybir.dt.float32
I32 = mybir.dt.int32

P = 128
N_NODES, N_EDGES = 6250, 200000
D, EF, GF, HID0, HID1 = 256, 96, 64, 1024, 512
BLOCKS = -(-N_NODES // P)
NP = BLOCKS * P
COLS = 4
GROUP = P * COLS
GROUPS = 8
STEP = GROUP * GROUPS
STEPS = BLOCKS
EP = STEPS * STEP
TILES = GROUPS * COLS
PAD_DEG = (EP - N_EDGES) // (NP - N_NODES)
WIN = 32
WIDE = 160
CHUNK = 8
FULL = 7
SLOTS = (FULL + 1) * CHUNK
SPLIT = 448
ROWS_CHECK = 112
COLS_CHECK = EP // ROWS_CHECK
FINE_RING = 8
SIGN_RING = 4
W0_PIECES = D // P + 3 + 2 + 1
ROWS_AHEAD = 14
SKIP = float(1 << 20)
BIG = 3.4028234663852886e38
LN_EPS = 1e-5
KC = D // P
HC0 = HID0 // P
HC1 = HID1 // P
assert TILES * WIN == HID0
assert SPLIT * SPLIT == EP and EP - N_EDGES == PAD_DEG * (NP - N_NODES) and STEPS % 2 == 1


class Step:

    def __init__(self, i, par, uses):
        self.i, self.par, self.uses = i, par, uses

    def next(self):
        return Step(self.i + 1, 1 - self.par, self.uses + self.par)

    def before(self):
        return Step(self.i - 1, 1 - self.par, self.uses - (1 - self.par))

    def first(self):
        return isinstance(self.i, int) and self.i == 0

    def last(self):
        return isinstance(self.i, int) and self.i == STEPS - 1


def at(n):
    return Step(n, n % 2, n // 2)


def wait(eng, sem, value):
    if isinstance(value, int) and value <= 0:
        return
    eng.wait_ge(sem, value)


def pipelined(eng, step, last):
    for n in range(4):
        step(at(n), at(n - 2) if n >= 2 else None)
    with eng.Fori(2, STEPS // 2) as it:
        step(Step(it * 2, 0, it), Step(it * 2 - 2, 0, it - 1))
        step(Step(it * 2 + 1, 1, it), Step(it * 2 - 1, 1, it - 1))
    step(at(STEPS - 1), at(STEPS - 3))
    last(at(STEPS - 2), at(STEPS - 1))


def each(one):
    def both(m, n):
        one(m)
        one(n)
    return both


def over_blocks(eng, one):
    one(at(0))
    with eng.Fori(1, BLOCKS // 2 + 1) as it:
        one(Step(it * 2 - 1, 1, it - 1))
        one(Step(it * 2, 0, it))


def build(nc, t):
    ctx = ExitStack()

    def sb(name, shape, dt=F32):
        return ctx.enter_context(nc.sbuf_tensor(name, shape, dt))

    def bank(name):
        return ctx.enter_context(nc.psum_tensor(name, [P, 512], F32))

    def sem(name):
        return ctx.enter_context(nc.semaphore(name))

    with ctx:
        x1_d = nc.dram_tensor("x1_d", [NP, D], F32).ap()
        rinv_d = nc.dram_tensor("rinv_d", [NP], F32).ap()

        w0x = sb("w0x", [P, KC, HID0])
        w0e = sb("w0e", [EF, 3, HID0])
        w0b = sb("w0b", [P, HC0, D])
        b2_0 = sb("b2_0", [P, D])
        bias0 = sb("bias0", [P, HC0])
        ident = sb("ident", [P, P])
        ones = sb("ones", [P, P])
        iota_f = sb("iota_f", [P, WIDE])
        eps_col = sb("eps_col", [P, 1])
        epsilon = sb("epsilon", [P, 1])
        start = sb("start", [P, BLOCKS + 1])
        idx_f = sb("idx_f", [P, BLOCKS, FULL + 1])
        full_cap = sb("full_cap", [P, BLOCKS, FULL])
        tail_cap = sb("tail_cap", [P, BLOCKS, CHUNK])
        rinv = sb("rinv", [P, BLOCKS])
        has = sb("has", [P, BLOCKS])
        wide_base = sb("wide_base", [1, STEPS], I32)
        place = sb("place", [P, STEPS * 2])
        base_f = sb("base_f", [P, STEPS * GROUPS])
        flag = sb("flag", [1, 1], I32)
        out1T = sb("out1T", [EF, NP])
        aggT = sb("aggT", [P, KC, NP])
        onehot = [sb(f"onehot{j}", [P, TILES, WIN]) for j in range(2)]
        select = [sb(f"select{j}", [P, 2, WIDE]) for j in range(2)]
        dst_t = [sb(f"dst_t{j}", [P, TILES], I32) for j in range(2)]
        w_t = [sb(f"w_t{j}", [P, TILES]) for j in range(2)]
        src_t = [sb(f"src_t{j}", [P, TILES], I32) for j in range(2)]
        dloc = sb("dloc", [P, TILES])
        hT = sb("hT", [P, HC0, P])
        xT_b = [sb(f"xT_b{j}", [P, KC, P]) for j in range(2)]
        xn_b = [sb(f"xn_b{j}", [P, D]) for j in range(2)]
        out_b = [sb(f"out_b{j}", [P, D]) for j in range(2)]
        z1 = sb("z1", [P, HID1])
        x2b = sb("x2b", [P, D])
        o1b = sb("o1b", [EF, P])
        o2b = sb("o2b", [EF, P])
        o3b = sb("o3b", [EF, P])
        rinv_b = [sb(f"rinv_b{j}", [EF, P]) for j in range(2)]
        chunk_max = sb("chunk_max", [P, FULL + 1, EF])
        max_w = sb("max_w", [P, EF])
        max_n = [sb(f"max_n{j}", [P, EF]) for j in range(2)]
        stats = sb("stats", [P, 6])
        mv = sb("mv", [P, 2])
        std = sb("std", [P, 1])
        rstd = sb("rstd", [P, 1])
        ell_idx = [sb(f"ell_idx{j}", [P, FULL + 1], I32) for j in range(2)]
        bad = sb("bad", [P, 5])
        bad_sum = sb("bad_sum", [P, 1])
        agg_in = sb("agg_in", [P, KC, P])

        ELL = SLOTS * EF
        NAT = TILES // 2 * EF
        ARENA = 2 * ELL + 2 * NAT
        arena = sb("arena", [P, ARENA])
        taken = [0]

        def piece(size, rows=P, dt=F32, of=arena, end=ARENA):
            lo = taken[0]
            taken[0] += -(-size // 8) * 8
            assert taken[0] <= end
            v = of[0:rows, lo:lo + size]
            return v if dt is F32 else v.bitcast(dt)

        ell = [piece(ELL) for j in range(2)]
        attr = [piece(NAT).rearrange("p (t f) -> p t f", f=EF) for j in range(2)]
        sums_nat = z1[:, D:D + 2 * EF]
        taken[0] = 0
        gath = [piece(COLS * D).rearrange("p (c d) -> p c d", d=D) for g in range(GROUPS)]
        w1T = piece(KC * HID1).rearrange("p (c h) -> p c h", c=KC)
        w2T = piece(HC1 * D).rearrange("p (c d) -> p c d", c=HC1)
        b1_1, g1_1, be1_1 = (piece(HID1) for _ in range(3))
        b2_1, g2_1, be2_1 = (piece(D) for _ in range(3))
        msg_nat = [piece(D) for half in range(2)]
        flat, room = aggT[:, :, :].rearrange("p c n -> p (c n)"), KC * NP
        taken[0] = 0

        def early(size, rows=P, dt=F32):
            return piece(size, rows, dt, flat, room)

        keys_i = early(SPLIT, dt=I32)
        dn_i = early(COLS_CHECK + 1, ROWS_CHECK, I32)
        disorder = early(COLS_CHECK, ROWS_CHECK)
        fine = [early(SPLIT) for j in range(FINE_RING)]
        signs = [early(SPLIT) for j in range(SIGN_RING)]
        u0 = early(1, GF)
        b1_0 = early(HC0)
        node_i = early(BLOCKS, dt=I32)
        node_f = early(BLOCKS)
        iota_i = early(WIDE, dt=I32)
        eights_i = early(CHUNK, dt=I32)
        eights_f = early(CHUNK)
        limit_i = early(BLOCKS - 1, 1, I32)
        limit_f = early(BLOCKS - 1, 1)
        base_b = early(STEPS * GROUPS, dt=I32)
        base_i = early(STEPS * GROUPS, 1, I32)
        place_i = early(STEPS * 2, dt=I32)
        lane = early(1)
        wide_f = early(STEPS)
        wide_span = early(STEPS, 1)
        ends_i = early(STEPS * GROUPS, 1, I32)
        span_f = early(STEPS * GROUPS, 1)
        coarse = early(BLOCKS)
        row_i = early(BLOCKS, dt=I32)
        in_row = early(BLOCKS)
        shift = early(P)
        wrap = early(P)
        nxt = early(BLOCKS)
        deg = early(BLOCKS)
        n_full = early(BLOCKS)
        tail_at = early(BLOCKS)
        rinvT = early(P, BLOCKS)
        late_f = early(BLOCKS - 1, 1)
        w0u = onehot[1][0:GF, :, :].rearrange("p t n -> p (t n)")
        flat, room = hT[:, :, :].rearrange("p c n -> p (c n)"), HID0
        taken[0] = 0
        full_f = early(BLOCKS * FULL).rearrange("p (b j) -> p b j", j=FULL)
        flat, room, taken[0] = z1, HID1, 0
        skipped = early(BLOCKS * FULL).rearrange("p (b j) -> p b j", j=FULL)
        flat, room, taken[0] = chunk_max[:, :, :].rearrange("p j f -> p (j f)"), (FULL + 1) * EF, 0
        by_slot = early(BLOCKS * CHUNK).rearrange("p (b j) -> p b j", j=CHUNK)
        taken[0] = 0
        out2T = piece(NP, EF)
        cntT = piece(NP, EF)
        g_attr = piece(EF)
        g_attrT = piece(P, EF)
        g_dst = piece(P, 1, I32)
        g_src = piece(1, dt=I32)
        g_w = piece(1)
        g_x = piece(D)
        g_xT = piece(KC * P).rearrange("p (c n) -> p c n", c=KC)
        g_one = piece(1, EF)

        seg = [bank("segA"), bank("segB")]
        hid = [bank("hidA"), bank("hidB")]
        zb = bank("zb")
        maxb = bank("maxb")
        wide = bank("wide")
        misc = bank("misc")

        keys_in, dn_in, win_in, u_in = sem("keys_in"), sem("dn_in"), sem("win_in"), sem("u_in")
        w0_in, eps_in, node_ready = sem("w0_in"), sem("eps_in"), sem("node_ready")
        rinv_in, tables_ready = [sem(f"rinv_in{j}") for j in range(2)], sem("tables_ready")
        rinv_ready, rinvT_ps, rinvT_ready, rinv_out = (
            sem("rinv_ready"), sem("rinvT_ps"), sem("rinvT_ready"), sem("rinv_out"))
        fine_in = [sem(f"fine_in{j}") for j in range(FINE_RING)]
        dst_in = [sem(f"dst_in{j}") for j in range(2)]
        attr_in = [sem(f"attr_in{j}") for j in range(2)]
        ell_in = [sem(f"ell_in{j}") for j in range(2)]
        x_in = [sem(f"x_in{j}") for j in range(2)]
        x1_out = [sem(f"x1_out{j}") for j in range(2)]
        w1_in = sem("w1_in")
        edge_in = [sem(f"edge_in{j}") for j in range(2)]
        gath_in = [sem(f"gath_in{g}") for g in range(GROUPS)]
        x1_in = [sem(f"x1_in{j}") for j in range(2)]
        y_out = [sem(f"y_out{j}") for j in range(2)]
        consts_ready, row_ready, count_ready = sem("consts_ready"), sem("row_ready"), sem("count_ready")
        fine_used, start_ready, nxt_ps = sem("fine_used"), sem("start_ready"), sem("nxt_ps")
        bias_ps, bad_ready = sem("bias_ps"), sem("bad_ready")
        bad_ps, setup_done, ident_zero = sem("bad_ps"), sem("setup_done"), sem("ident_zero")
        ell_clear = sem("ell_clear")
        onehot_ready, seg_ps, seg_added = sem("onehot_ready"), sem("seg_ps"), sem("seg_added")
        dst_float, dst_local, select_ready = sem("dst_float"), sem("dst_local"), sem("select_ready")
        dist_ready, dist_squared = sem("dist_ready"), sem("dist_squared")
        sums_copied, sumsT_ps = sem("sums_copied"), sem("sumsT_ps")
        ell_idx_ready, ell_used, max_ready = sem("ell_idx_ready"), sem("ell_used"), sem("max_ready")
        maxT_ps, hid_ps, z_ps = sem("maxT_ps"), sem("hid_ps"), sem("z_ps")
        o1_ready, o2_ready, relu_ready, std_ready = (
            sem("o1_ready"), sem("o2_ready"), sem("relu_ready"), sem("std_ready"))
        mean_ready, var_ready, x1_ready = sem("mean_ready"), sem("var_ready"), sem("x1_ready")
        wonehot_ready, msg_ps, msg_added = sem("wonehot_ready"), sem("msg_ps"), sem("msg_added")
        select1_ready, msg_copied, msgT_ps = sem("select1_ready"), sem("msg_copied"), sem("msgT_ps")
        x1T_ps, agg_ready, h1_ps, h1_ready, h1T_ps, h1T_ready, h2_ps = (
            sem("x1T_ps"), sem("agg_ready"), sem("h1_ps"), sem("h1_ready"), sem("h1T_ps"), sem("h1T_ready"),
            sem("h2_ps"))
        h1_var, out_var, y_var = sem("h1_var"), sem("out_var"), sem("y_var")
        h1_std, out_std, y_std, y_ready = sem("h1_std"), sem("out_std"), sem("y_std"), sem("y_ready")
        g_attr_in, g_dst_in, g_src_in, g_w_in, g_gath_in = (
            sem("g_attr_in"), sem("g_dst_in"), sem("g_src_in"), sem("g_w_in"), sem("g_gath_in"))
        g_turned, g_scaled, g_done, g_sums = (
            sem("g_turned"), sem("g_scaled"), sem("g_done"), sem("g_sums"))

        GT = EP // P
        block = ctx.enter_context(nc.Block())

        def is_fast(eng):
            eng.wait_ge(setup_done, 1)
            return eng.value_load(flag[0:1, 0:1], min_val=0, max_val=1) < 1

        @block.sync
        def _(sp):
            sp.dma_start(keys_i, t["keys"].partition_broadcast(P)).then_inc(keys_in, 16)
            sp.dma_start(base_b, t["base"].partition_broadcast(P)).then_inc(win_in, 16)
            sp.dma_start(base_i, t["base"].unsqueeze(0)).then_inc(win_in, 16)
            sp.dma_start(ends_i, t["ends"].unsqueeze(0)).then_inc(win_in, 16)
            sp.dma_start(place_i, t["place"]).then_inc(win_in, 16)
            sp.dma_start(lane, t["lane"]).then_inc(win_in, 16)
            sp.dma_start(w0u, t["W1"][D + 3 * EF:, :]).then_inc(u_in, 16)
            sp.dma_start(u0, t["u0"]).then_inc(u_in, 16)
            sp.dma_start(b1_0, t["b1_0"]).then_inc(u_in, 16)
            sp.dma_start(epsilon[:, :], t["epsilon"].to_broadcast([P, 1])).then_inc(eps_in, 16)
            sp.dma_start(dn_i, t["dst_rows"]).then_inc(dn_in, 16)

            def load_edges(s):
                wait(sp, dist_ready, s.i - 1)
                sp.dma_start(dst_t[s.par][:, :], t["dst_s"][bass.ds(s.i, 1), :, :]
                             .rearrange("a p t -> (a p) t")).then_inc(dst_in[s.par], 16)
                for half in range(2):
                    wait(sp, seg_ps, s.i * 2 - 1 + half)
                    rows = t["attr"].rearrange("(s g p c) f -> s p g (c f)", g=GROUPS, p=P, c=COLS)
                    sp.dma_start(attr[half].rearrange("p (g c) f -> p g (c f)", c=COLS),
                                 rows[bass.ds(s.i, 1), :, half * 4:half * 4 + 4, :]
                                 .rearrange("a p g r -> (a p) g r")).then_inc(attr_in[half], 16)

            pieces = ([(w0x[:, c, :], t["W1"][c * P:(c + 1) * P, :]) for c in range(KC)]
                      + [(w0e[:, c, :], t["W1"][D + c * EF:D + (c + 1) * EF, :]) for c in range(3)]
                      + [(w0b[:, c:c + HC0 // 2, :], t["W2"][c * P:(c + HC0 // 2) * P, :]
                          .rearrange("(c p) d -> p c d", p=P)) for c in range(0, HC0, HC0 // 2)]
                      + [(b2_0[:, :], t["b2_0"].partition_broadcast(P))])
            assert len(pieces) == W0_PIECES
            for n, (out, rows) in enumerate(pieces):
                sp.wait_ge(fine_used, 4 * n + 4)
                sp.dma_start(out, rows).then_inc(w0_in, 16)
            sp.wait_ge(fine_used, BLOCKS - 2)
            load_edges(at(0))

            def load_x(m):
                wait(sp, z_ps, m.i - 1)
                wait(sp, var_ready, m.i - 1)
                sp.dma_start(xT_b[m.par][:, :, :], t["xT"].rearrange("(c p) n -> p c n", p=P)
                             [:, :, bass.ds(m.i * P, P)]).then_inc(x_in[m.par], 16)
                sp.dma_start(xn_b[m.par][:, :], t["x"][bass.ds(m.i * P, P), :]).then_inc(x_in[m.par], 16)

            def load_rinv(m):
                wait(sp, mean_ready, m.i - 1)
                sp.dma_start(rinv_b[m.par][:, :], rinv_d[bass.ds(m.i * P, P)].partition_broadcast(EF)
                             ).then_inc(rinv_in[m.par], 16)

            def last1(m):
                load_rinv(m)
                load_x(m)

            def phase1(s, m):
                if s.first():
                    sp.wait_ge(rinvT_ready, 1)
                    sp.dma_start(rinv_d.rearrange("(b p) -> b p", p=P), rinvT).then_inc(rinv_out, 16)
                else:
                    load_edges(s)
                if m is None:
                    sp.wait_ge(rinv_out, 16)
                else:
                    load_rinv(m)
                    load_x(m)

            def load_second_layer():
                for out, name in ((w1T, "w1T"), (w2T, "w2T")):
                    sp.dma_start(out, t[name].rearrange("(c p) n -> p c n", p=P)).then_inc(w1_in, 16)
                for out, name in ((b1_1, "b1_1"), (g1_1, "g1_1"), (be1_1, "be1_1"),
                                  (b2_1, "b2_1"), (g2_1, "g2_1"), (be2_1, "be2_1")):
                    sp.dma_start(out, t[name].partition_broadcast(P)).then_inc(w1_in, 16)

            def all_x1(eng):
                for j in range(2):
                    eng.wait_ge(x1_out[j], 16 * ((BLOCKS + 1 - j) // 2))

            def load_x1(m):
                wait(sp, y_ready, m.i - 1)
                sp.dma_start(xn_b[m.par][:, :], x1_d[bass.ds(m.i * P, P), :]).then_inc(x1_in[m.par], 16)

            def phase2(s, m):
                wait(sp, msg_ps, (s.i - 1) * GROUPS)
                wait(sp, wonehot_ready, s.i - 1)
                for out, name in ((src_t, "src_s"), (dst_t, "dst_s"), (w_t, "w_s")):
                    sp.dma_start(out[s.par][:, :], t[name][bass.ds(s.i, 1), :, :]
                                 .rearrange("a p t -> (a p) t")).then_inc(edge_in[s.par], 16)
                if m is not None:
                    load_x1(m)
                elif s.i == 1:
                    sp.wait_ge(var_ready, BLOCKS)
                    all_x1(sp)

            with sp.If(is_fast(sp)):
                pipelined(sp, phase1, each(last1))
                sp.wait_ge(ell_used, STEPS)
                sp.wait_ge(seg_ps, 2 * STEPS)
                load_second_layer()
                pipelined(sp, phase2, each(load_x1))
            with sp.Else():
                for half in range(2):
                    sp.wait_ge(attr_in[half], 16)
                sp.wait_ge(ell_clear, 2)
                with sp.Fori(0, GT) as k:
                    sp.wait_ge(g_done, k)
                    sp.dma_start(g_attr, t["attr"][bass.ds(k * P, P), :]).then_inc(g_attr_in, 16)
                    sp.dma_start(g_dst, t["dst_f"][bass.ds(k, 1), :]).then_inc(g_dst_in, 16)
                over_blocks(sp, load_x)
                all_x1(sp)
                with sp.Fori(0, GT) as k:
                    sp.wait_ge(g_done, k + GT)
                    sp.dma_start(g_src, t["src_f"][bass.ds(k * P, P), :]).then_inc(g_src_in, 16)
                    sp.dma_start(g_w, t["w_f"][bass.ds(k * P, P), :]).then_inc(g_w_in, 16)
                    sp.dma_start(g_dst, t["dst_f"][bass.ds(k, 1), :]).then_inc(g_dst_in, 16)
                sp.wait_ge(g_done, 2 * GT)
                load_second_layer()
                over_blocks(sp, load_x1)

        @block.gpsimd
        def _(pool):
            pool.iota(node_i, pattern=[[P, BLOCKS]], base=0, channel_multiplier=1).then_inc(consts_ready, 1)
            pool.iota(iota_i, pattern=[[1, WIDE]], base=0, channel_multiplier=0).then_inc(consts_ready, 1)
            pool.iota(eights_i, pattern=[[CHUNK, CHUNK]], base=0, channel_multiplier=0).then_inc(consts_ready, 1)
            pool.iota(limit_i, pattern=[[STEP, BLOCKS - 1]], base=2 * STEP, channel_multiplier=0).then_inc(consts_ready, 1)
            pool.memset(ident[:, :], 0.0).then_inc(ident_zero, 1)
            pool.memset(shift, 0.0).then_inc(ident_zero, 1)
            pool.memset(wrap, 0.0).then_inc(ident_zero, 1)
            pool.wait_ge(ident_zero, 3)
            pool.affine_select(out=ident[:, :], in_=ident[:, :], compare_op=ALU.not_equal, fill=1.0,
                               base=0, pattern=[[-1, P]], channel_multiplier=1).then_inc(consts_ready, 1)
            pool.affine_select(out=shift, in_=shift, compare_op=ALU.not_equal, fill=1.0,
                               base=-1, pattern=[[-1, P]], channel_multiplier=1).then_inc(consts_ready, 1)
            pool.memset(wrap[0:1, P - 1:P], 1.0).then_inc(consts_ready, 1)
            pool.memset(ones[:, :], 1.0).then_inc(consts_ready, 1)
            pool.memset(eps_col[:, :], LN_EPS).then_inc(consts_ready, 1)
            bound = pool.alloc_register("bound")
            pool.reg_mov(bound, EP)

            def wait_for_bound(sem_, value, last_row):
                wait(pool, sem_, value)
                pool.reg_alu(bound, bound, last_row, ALU.min)
                return pool.snap(bound, min_val=0, max_val=last_row)

            def distances(s):
                wait_for_bound(dst_in[s.par], s.uses * 16 + 16, EP - CHUNK)
                pool.tensor_copy(dloc[:, :], dst_t[s.par][:, :]).then_inc(dst_float, 1)
                pool.wait_ge(dst_float, s.i + 1)
                pool.tensor_tensor(dloc[:, :].rearrange("p (g c) -> p g c", c=COLS),
                                   dloc[:, :].rearrange("p (g c) -> p g c", c=COLS),
                                   base_f[:, bass.ds(s.i * GROUPS, GROUPS)].unsqueeze(2)
                                   .to_broadcast([P, GROUPS, COLS]), ALU.subtract).then_inc(dst_local, 1)
                wait_for_bound(dst_local, s.i + 1, EP - CHUNK)
                wait(pool, seg_ps, (s.i - 1) * 2)
                pool.tensor_tensor(onehot[s.par][:, :, :], dloc[:, :].unsqueeze(2).to_broadcast([P, TILES, WIN]),
                                   iota_f[:, 0:WIN].unsqueeze(1).to_broadcast([P, TILES, WIN]),
                                   ALU.subtract).then_inc(dist_ready, 1)
                wait_for_bound(dist_ready, s.i + 1, EP - CHUNK)

            for b in range(BLOCKS):
                pool.wait_ge(row_ready, b + 1)
                if b >= FINE_RING:
                    pool.wait_ge(fine_used, b - FINE_RING + 1)
                pool.indirect_dma_start(fine[b % FINE_RING].bitcast(I32), None, t["dst_split"],
                                        bass.IndirectOffsetOnAxis(ap=row_i[:, b:b + 1], axis=0),
                                        bounds_check=SPLIT - 1, oob_is_err=False
                                        ).then_inc(fine_in[b % FINE_RING], 16)
            pool.wait_ge(tables_ready, 1)
            distances(at(0))

            def phase1(s, m):
                wait(pool, ell_used, s.i - 1)
                pool.tensor_copy(ell_idx[s.par][:, :], idx_f[:, bass.ds(s.i, 1), :]
                                 .rearrange("p a j -> p (a j)")).then_inc(ell_idx_ready, 1)
                if s.first() or m is None:
                    pool.wait_ge(ell_clear, s.i + 1)
                last_row = wait_for_bound(ell_idx_ready, s.i + 1, EP - CHUNK)
                for j in range(FULL + 1):
                    pool.indirect_dma_start(ell[s.par][:, j * CHUNK * EF:(j + 1) * CHUNK * EF], None,
                                            t["attr"], bass.IndirectOffsetOnAxis(
                                                ap=ell_idx[s.par][:, j:j + 1], axis=0),
                                            bounds_check=last_row, oob_is_err=False
                                            ).then_inc(ell_in[s.par], 16)
                if not s.last():
                    distances(s.next())

            def phase2(s, m):
                pool.wait_ge(edge_in[s.par], s.uses * 48 + 48)
                for g in range(GROUPS):
                    last_row = wait_for_bound(msg_ps, (s.i - 1) * GROUPS + g + 1, NP - 1)
                    for c in range(COLS):
                        pool.indirect_dma_start(gath[g][:, c, :], None, x1_d,
                                                bass.IndirectOffsetOnAxis(
                                                    ap=src_t[s.par][:, g * COLS + c:g * COLS + c + 1], axis=0),
                                                bounds_check=last_row, oob_is_err=False
                                                ).then_inc(gath_in[g], 16)

            def all_x1():
                for j in range(2):
                    pool.wait_ge(x1_out[j], 16 * ((BLOCKS + 1 - j) // 2))

            with pool.If(is_fast(pool)):
                pipelined(pool, phase1, lambda m, n: None)
                all_x1()
                pool.wait_ge(ell_used, STEPS)
                pool.wait_ge(seg_ps, 2 * STEPS)
                pipelined(pool, phase2, lambda m, n: None)
            with pool.Else():
                all_x1()
                with pool.Fori(0, GT) as k:
                    last_row = wait_for_bound(g_src_in, k * 16 + 16, NP - 1)
                    pool.indirect_dma_start(g_x, None, x1_d, bass.IndirectOffsetOnAxis(ap=g_src, axis=0),
                                            bounds_check=last_row, oob_is_err=False).then_inc(g_gath_in, 16)
                    pool.wait_ge(g_gath_in, k * 16 + 16)

        @block.tensor
        def _(pe):
            pe.wait_ge(consts_ready, 9)
            pe.wait_ge(u_in, 48)
            for c in range(HC0):
                mm = pe.matmul(misc[:, c:c + 1], w0u[:, c * P:(c + 1) * P], u0, start=True, stop=True)
            mm.then_inc(bias_ps, 1)
            pe.wait_ge(start_ready, 1)
            pe.matmul(zb[:, 0:BLOCKS], shift, start[:, 0:BLOCKS], start=True, stop=False)
            pe.matmul(zb[:, 0:BLOCKS], wrap, start[:, 1:BLOCKS + 1], start=False, stop=True).then_inc(nxt_ps, 1)
            pe.wait_ge(rinv_ready, 1)
            pe.transpose(zb[0:BLOCKS, P:2 * P], rinv[:, :], ident[:, :]).then_inc(rinvT_ps, 1)
            pe.wait_ge(bad_ready, 1)
            pe.matmul(maxb[0:1, 0:1], bad_sum[:, :], ones[:, 0:1], start=True, stop=True).then_inc(bad_ps, 1)

            def sums(s):
                pe.wait_ge(onehot_ready, s.i + 1)
                wait(pe, sums_copied, s.i)
                for half in range(2):
                    pe.wait_ge(attr_in[half], s.i * 16 + 16)
                    for c in range(COLS):
                        for g in range(GROUPS // 2):
                            mm = pe.matmul(seg[0][g * WIN:(g + 1) * WIN, half * EF:(half + 1) * EF],
                                           onehot[s.par][:, half * 16 + g * COLS + c, :],
                                           attr[half][:, g * COLS + c, :],
                                           start=(c == 0), stop=(c == COLS - 1))
                    mm.then_inc(seg_ps, 1)

            def turn_sums(s):
                pe.wait_ge(select_ready, s.i + 1)
                pe.wait_ge(sums_copied, s.i + 1)
                wait(pe, seg_added, s.i)
                for half in range(2):
                    mm = pe.matmul(seg[1][0:EF, 0:WIDE], sums_nat[:, half * EF:(half + 1) * EF],
                                   select[s.par][:, half, :], start=(half == 0), stop=(half == 1))
                mm.then_inc(sumsT_ps, 1)

            def hidden(m, parts, first, last):
                for half in range(2):
                    for c in range(HC0 // 2):
                        h = half * (HC0 // 2) + c
                        for n, (w, x) in enumerate(parts):
                            mm = pe.matmul(hid[half][:, c * P:(c + 1) * P], w[:, h * P:(h + 1) * P], x,
                                           start=(first and c == 0 and n == 0),
                                           stop=(last and n == len(parts) - 1), skip_group_check=True)
                    if last:
                        mm.then_inc(hid_ps, 1)

            def turn_max(m):
                pe.wait_ge(max_ready, m.i + 1)
                wait(pe, o2_ready, m.i)
                pe.transpose(maxb[0:EF, 0:P], max_n[m.par][:, :], ident[:, :]).then_inc(maxT_ps, 1)

            def hidden_of_x(m):
                if m.first():
                    pe.wait_ge(w0_in, 16 * W0_PIECES)
                wait(pe, relu_ready, m.i * 2)
                pe.wait_ge(x_in[m.par], m.uses * 32 + 32)
                hidden(m, [(w0x[:, k, :], xT_b[m.par][:, k, :]) for k in range(KC)], True, False)

            def hidden_of_edges(m):
                pe.wait_ge(o1_ready, m.i + 1)
                pe.wait_ge(o2_ready, m.i + 1)
                pe.wait_ge(mean_ready, m.i + 1)
                hidden(m, [(w0e[:, 0, :], o1b[:, :]), (w0e[:, 1, :], o2b[:, :]), (w0e[:, 2, :], o3b[:, :])],
                       False, True)

            def second(m):
                wait(pe, var_ready, m.i)
                for c in range(HC0):
                    if c % (HC0 // 2) == 0:
                        pe.wait_ge(relu_ready, m.i * 2 + 1 + c // (HC0 // 2))
                    mm = pe.matmul(zb[:, 0:D], hT[:, c, :], w0b[:, c, :], start=(c == 0), stop=(c == HC0 - 1))
                mm.then_inc(z_ps, 1)

            def mlp0(m):
                hidden_of_x(m)
                hidden_of_edges(m)
                second(m)

            def phase1(s, m):
                sums(s)
                if m is not None:
                    hidden_of_x(m)
                    turn_max(m)
                turn_sums(s)
                if m is not None:
                    hidden_of_edges(m)
                    second(m)

            def last1(m):
                hidden_of_x(m)
                turn_max(m)
                hidden_of_edges(m)
                second(m)

            def messages(s, g):
                half, q = g // 4, g % 4
                if q == 0:
                    wait(pe, msg_copied, s.i * 2 - 1 + half)
                pe.wait_ge(gath_in[g], s.i * 16 * COLS + 16 * COLS)
                for c in range(COLS):
                    mm = pe.matmul(seg[half][q * WIN:(q + 1) * WIN, 0:D], onehot[s.par][:, g * COLS + c, :],
                                   gath[g][:, c, :], start=(c == 0), stop=(c == COLS - 1))
                mm.then_inc(msg_ps, 1)

            def turn_messages(s):
                pe.wait_ge(select1_ready, s.i + 1)
                pe.wait_ge(msg_copied, s.i * 2 + 2)
                wait(pe, msg_added, s.i)
                for k in range(KC):
                    for half in range(2):
                        mm = pe.matmul(wide[:, k * WIDE:(k + 1) * WIDE], msg_nat[half][:, k * P:(k + 1) * P],
                                       select[s.par][:, half, :], start=(half == 0), stop=(half == 1))
                mm.then_inc(msgT_ps, 1)

            def turn_x1(m):
                pe.wait_ge(x1_in[m.par], m.uses * 16 + 16)
                wait(pe, agg_ready, m.i)
                for c in range(KC):
                    mm = pe.transpose(misc[:, c * P:(c + 1) * P], xn_b[m.par][:, c * P:(c + 1) * P], ident[:, :])
                mm.then_inc(x1T_ps, 1)

            def first1(m):
                pe.wait_ge(agg_ready, m.i + 1)
                wait(pe, h1_var, m.i)
                for k in range(KC):
                    mm = pe.matmul(hid[0][:, :], agg_in[:, k, :], w1T[:, k, :], start=(k == 0), stop=(k == KC - 1))
                mm.then_inc(h1_ps, 1)

            def turn_h1(m):
                pe.wait_ge(h1_ready, m.i + 1)
                wait(pe, h1T_ready, m.i)
                for c in range(HC1):
                    mm = pe.transpose(hid[1][:, c * P:(c + 1) * P], z1[:, c * P:(c + 1) * P], ident[:, :])
                mm.then_inc(h1T_ps, 1)

            def second1(m):
                pe.wait_ge(h1T_ready, m.i + 1)
                wait(pe, out_var, m.i)
                for c in range(HC1):
                    mm = pe.matmul(zb[:, 0:D], hT[:, c, :], w2T[:, c, :], start=(c == 0), stop=(c == HC1 - 1))
                mm.then_inc(h2_ps, 1)

            def mlp1(m):
                turn_x1(m)
                first1(m)
                turn_h1(m)
                second1(m)

            def last2(m, n):
                turn_x1(m)
                first1(m)
                turn_x1(n)
                turn_h1(m)
                first1(n)
                second1(m)
                turn_h1(n)
                second1(n)

            def phase2(s, m):
                pe.wait_ge(wonehot_ready, s.i + 1)
                for g in range(GROUPS):
                    messages(s, g)
                    if g == 0 and m is not None:
                        turn_x1(m)
                    if g == 1 and m is not None:
                        first1(m)
                    if g == 3 and m is not None:
                        turn_h1(m)
                    if g == 5 and m is not None:
                        second1(m)
                turn_messages(s)

            with pe.If(is_fast(pe)):
                pipelined(pe, phase1, each(last1))
                pe.wait_ge(w1_in, 16 * 8)
                pipelined(pe, phase2, last2)
            with pe.Else():
                with pe.Fori(0, GT) as k:
                    pe.wait_ge(g_attr_in, k * 16 + 16)
                    pe.transpose(misc[0:EF, 0:P], g_attr, ident[:, :]).then_inc(g_turned, 1)
                over_blocks(pe, mlp0)
                with pe.Fori(0, GT) as k:
                    pe.wait_ge(g_scaled, k + 1)
                    for c in range(KC):
                        mm = pe.transpose(misc[:, c * P:(c + 1) * P], g_x[:, c * P:(c + 1) * P], ident[:, :])
                    mm.then_inc(g_turned, 1)
                pe.wait_ge(w1_in, 16 * 8)
                over_blocks(pe, mlp1)

        @block.scalar
        def _(act):
            def deviation(m, have, want):
                act.wait_ge(have, m.i + 1)
                act.activation(std[:, :], mv[:, 1:2], ACT.Sqrt, bias=eps_col[:, 0:1]).then_inc(want, 1)

            def sums_in(m, fast):
                if fast:
                    act.wait_ge(seg_added, STEPS if m.last() else m.i + 2)
                wait(act, hid_ps, m.i * 2)
                wait(act, mean_ready, m.i)
                act.activation(o1b[:, :], out1T[:, bass.ds(m.i * P, P)], ACT.Copy).then_inc(o1_ready, 1)

            def maxima_in(m, fast):
                wait(act, hid_ps, m.i * 2)
                if fast:
                    act.wait_ge(maxT_ps, m.i + 1)
                    act.activation(o2b[:, :], maxb[0:EF, 0:P], ACT.Copy).then_inc(o2_ready, 1)
                else:
                    act.activation(o2b[:, :], out2T[:, bass.ds(m.i * P, P)], ACT.Copy).then_inc(o2_ready, 1)

            def copy_sums(s):
                act.wait_ge(seg_ps, s.i * 2 + 2)
                wait(act, sumsT_ps, s.i)
                act.activation(sums_nat, seg[0][:, 0:2 * EF], ACT.Copy).then_inc(sums_copied, 1)

            def mlp0(m, fast):
                wait(act, z_ps, m.i)
                for c in range(HC0):
                    half, q = c // (HC0 // 2), c % (HC0 // 2)
                    if q == 0:
                        act.wait_ge(hid_ps, m.i * 2 + 1 + half)
                    relu = act.activation(hT[:, c, :], hid[half][:, q * P:(q + 1) * P], ACT.Relu,
                                          bias=bias0[:, c:c + 1])
                    if q == HC0 // 2 - 1:
                        relu.then_inc(relu_ready, 1)
                if fast and not m.last():
                    sums_in(m.next(), True)

            def store_x1(m):
                deviation(m, var_ready, std_ready)
                act.wait_ge(x1_ready, m.i + 1)
                act.dma_start(x1_d[bass.ds(m.i * P, P), :], out_b[m.par][:, :]).then_inc(x1_out[m.par], 16)

            def window_matrix(s):
                act.wait_ge(dist_ready, s.i + 1)
                act.activation(onehot[s.par][:, :, :], onehot[s.par][:, :, :], ACT.Square
                               ).then_inc(dist_squared, 1)
                act.wait_ge(dist_squared, s.i + 1)
                act.activation(onehot[s.par][:, :, :], onehot[s.par][:, :, :], ACT.Relu,
                               bias=ones[:, 0:1], scale=-1.0).then_inc(onehot_ready, 1)

            def phase1(s, m):
                copy_sums(s)
                if m is not None:
                    maxima_in(m, True)
                    if isinstance(s.i, int) and s.i == 3:
                        store_x1(m.before())
                if not s.last():
                    window_matrix(s.next())
                if m is None and s.i == 1:
                    sums_in(at(0), True)
                if m is not None:
                    mlp0(m, True)
                    if not m.first():
                        store_x1(m)

            def block0(m, fast):
                if not fast:
                    sums_in(m, False)
                maxima_in(m, fast)
                mlp0(m, fast)
                store_x1(m)

            def copy_messages(s, half):
                act.wait_ge(msg_ps, s.i * GROUPS + half * 4 + 4)
                wait(act, msgT_ps, s.i)
                act.activation(msg_nat[half], seg[half][:, 0:D], ACT.Copy).then_inc(msg_copied, 1)

            def second1(m):
                act.wait_ge(h1T_ps, m.i + 1)
                wait(act, h2_ps, m.i)
                act.activation(hT[:, 0:HC1, :], hid[1][:, :].rearrange("p (c n) -> p c n", c=HC1),
                               ACT.Relu).then_inc(h1T_ready, 1)

            def finish1(m):
                deviation(m, out_var, out_std)
                deviation(m, y_var, y_std)
                act.wait_ge(y_ready, m.i + 1)
                act.dma_start(t["y"][bass.ds(m.i * P, P), :], out_b[m.par][:, :]).then_inc(y_out[m.par], 16)

            def mlp1(m):
                deviation(m, h1_var, h1_std)
                second1(m)
                finish1(m)

            def last2(m, n):
                deviation(m, h1_var, h1_std)
                second1(m)
                deviation(n, h1_var, h1_std)
                finish1(m)
                second1(n)
                finish1(n)

            def phase2(s, m):
                if m is not None:
                    deviation(m, h1_var, h1_std)
                copy_messages(s, 0)
                if m is not None:
                    second1(m)
                    finish1(m)
                copy_messages(s, 1)

            act.wait_ge(keys_in, 16)
            act.wait_ge(node_ready, 1)
            for b in range(BLOCKS):
                wait(act, count_ready, b - SIGN_RING + 1)
                act.activation(signs[b % SIGN_RING][:, 1:SPLIT], keys_i[:, 1:SPLIT], ACT.Sign, scale=-1.0,
                               bias=node_f[:, b:b + 1], accum_out=coarse[:, b:b + 1]).then_inc(count_ready, 1)

            act.wait_ge(rinvT_ps, 1)
            act.activation(rinvT, zb[0:BLOCKS, P:2 * P], ACT.Copy).then_inc(rinvT_ready, 1)
            with act.If(is_fast(act)):
                window_matrix(at(0))
                pipelined(act, phase1, each(lambda m: block0(m, True)))
                pipelined(act, phase2, last2)
            with act.Else():
                act.wait_ge(g_sums, 1)
                over_blocks(act, lambda m: block0(m, False))
                act.wait_ge(g_done, 2 * GT)
                over_blocks(act, mlp1)
            for j in range(2):
                act.wait_ge(y_out[j], 16 * ((BLOCKS + 1 - j) // 2))

        @block.vector
        def _(dve):
            tt, ts, red = dve.tensor_tensor, dve.tensor_scalar, dve.tensor_reduce

            def settle():
                dve.drain()

            dve.memset(start[:, BLOCKS:BLOCKS + 1], float(EP))
            dve.memset(bad[:, :], 0.0)
            dve.wait_ge(consts_ready, 1)
            ts(node_f, node_i, -0.5, None, ALU.add).then_inc(node_ready, 1)

            def order_check():
                dve.wait_ge(dn_in, 16)
                tt(disorder, dn_i[:, 0:COLS_CHECK], dn_i[:, 1:COLS_CHECK + 1], ALU.is_gt)
                settle()
                red(bad[0:ROWS_CHECK, 0:1], disorder, AX.X, ALU.add)

            def window_check():
                dve.wait_ge(win_in, 80)
                tt(span_f, ends_i, base_i, ALU.subtract)
                ts(wide_f, base_b.rearrange("p (s g) -> p g s", g=GROUPS)[:, 0, :], float(NP - WIDE), None, ALU.min)
                ts(place[:, :], place_i, lane, None, ALU.add)
                dve.tensor_copy(base_f[:, :], base_b)
                dve.wait_ge(consts_ready, 4)
                dve.tensor_copy(eights_f, eights_i)
                dve.tensor_copy(limit_f, limit_i)
                dve.tensor_copy(iota_f[:, :], iota_i).then_inc(tables_ready, 1)
                settle()
                tt(wide_span, ends_i.rearrange("p (s g) -> p g s", g=GROUPS)[:, GROUPS - 1, :], wide_f[0:1, :],
                   ALU.subtract)
                dve.tensor_copy(wide_base[:, :], wide_f[0:1, :])
                tt(place[:, :].rearrange("p (s h) -> p s h", h=2), place[:, :].rearrange("p (s h) -> p s h", h=2),
                   wide_f.unsqueeze(2).to_broadcast([P, STEPS, 2]), ALU.subtract)
                ts(span_f, span_f, float(WIN), None, ALU.is_ge)
                settle()
                ts(wide_span, wide_span, float(WIDE), None, ALU.is_ge)
                settle()
                red(bad[0:1, 1:2], span_f, AX.X, ALU.add)
                red(bad[0:1, 4:5], wide_span, AX.X, ALU.add)

            for b in range(BLOCKS + ROWS_AHEAD):
                if b < BLOCKS:
                    dve.wait_ge(count_ready, b + 1)
                    ts(row_i[:, b:b + 1], coarse[:, b:b + 1], 0.5, (SPLIT - 1) / 2, ALU.mult, ALU.add
                       ).then_inc(row_ready, 1)
                if b >= ROWS_AHEAD:
                    d = b - ROWS_AHEAD
                    dve.wait_ge(fine_in[d % FINE_RING], 16 * (d // FINE_RING + 1))
                    ts(fine[d % FINE_RING], fine[d % FINE_RING].bitcast(I32), node_f[:, d:d + 1], None, ALU.is_lt,
                       ALU.add, accum_out=in_row[:, d:d + 1]).then_inc(fine_used, 1)
                    if d == 4:
                        dve.memset(ell[0][:, 0:ELL // 2], 0.0)
                    if d == 10:
                        dve.memset(ell[0][:, ELL // 2:], 0.0).then_inc(ell_clear, 1)
                    if d == 16:
                        order_check()
                    if d == 32:
                        window_check()
            ts(coarse, coarse, 0.5, (SPLIT - 1) / 2, ALU.mult, ALU.add)
            settle()
            dve.scalar_tensor_tensor(out=start[:, 0:BLOCKS], in0=coarse, scalar=float(SPLIT), in1=in_row,
                                     op0=ALU.mult, op1=ALU.add).then_inc(start_ready, 1)
            settle()
            tt(late_f, start[0:1, 1:BLOCKS], limit_f, ALU.is_gt)
            settle()
            red(bad[0:1, 2:3], late_f, AX.X, ALU.add)

            dve.wait_ge(nxt_ps, 1)
            dve.tensor_copy(nxt, zb[:, 0:BLOCKS])
            settle()
            tt(deg, nxt, start[:, 0:BLOCKS], ALU.subtract)
            settle()
            ts(n_full, deg, float(SLOTS), None, ALU.is_gt)
            tt(full_f, deg.unsqueeze(2).to_broadcast([P, BLOCKS, FULL]),
               eights_f[:, 1:CHUNK].unsqueeze(1).to_broadcast([P, BLOCKS, FULL]), ALU.is_gt)
            ts(rinv[:, :], deg, 1.0, None, ALU.max)
            ts(has[:, :], deg, 1.0, None, ALU.min)
            settle()
            red(bad[:, 3:4], n_full, AX.X, ALU.add)
            dve.reciprocal(rinv[:, :], rinv[:, :]).then_inc(rinv_ready, 1)
            settle()
            red(bad_sum[:, :], bad[:, :], AX.X, ALU.add).then_inc(bad_ready, 1)
            red(n_full, full_f, AX.X, ALU.add)
            tt(idx_f[:, :, 0:FULL], start[:, 0:BLOCKS].unsqueeze(2).to_broadcast([P, BLOCKS, FULL]),
               eights_f[:, 0:FULL].unsqueeze(1).to_broadcast([P, BLOCKS, FULL]), ALU.add)
            ts(skipped, full_f, -SKIP, SKIP, ALU.mult, ALU.add)
            settle()
            tt(idx_f[:, :, 0:FULL], idx_f[:, :, 0:FULL], skipped, ALU.add)
            dve.scalar_tensor_tensor(out=tail_at, in0=n_full, scalar=float(CHUNK), in1=start[:, 0:BLOCKS],
                                     op0=ALU.mult, op1=ALU.add)
            dve.wait_ge(eps_in, 16)
            dve.wait_ge(bias_ps, 1)
            tt(bias0[:, :], misc[:, 0:HC0], b1_0, ALU.add)
            dve.wait_ge(bad_ps, 1)
            ts(flag[:, :], maxb[0:1, 0:1], 1.0, None, ALU.min)
            settle()
            ts(idx_f[:, :, FULL:FULL + 1], tail_at.unsqueeze(2), float(EP - CHUNK), None, ALU.min
               ).then_inc(setup_done, 1)
            dve.memset(ell[1], 0.0).then_inc(ell_clear, 1)
            ts(full_cap[:, :, :], full_f, 0.5, 2.0, ALU.subtract, ALU.mult)
            ts(eights_f, eights_f, 1.0 / CHUNK, None, ALU.mult)
            settle()
            ts(full_cap[:, :, :], full_cap[:, :, :], BIG, None, ALU.mult)
            tt(by_slot, idx_f[:, :, FULL:FULL + 1].to_broadcast([P, BLOCKS, CHUNK]),
               eights_f.unsqueeze(1).to_broadcast([P, BLOCKS, CHUNK]), ALU.add)
            settle()
            tt(tail_cap[:, :, :], by_slot, tail_at.unsqueeze(2).to_broadcast([P, BLOCKS, CHUNK]), ALU.is_ge)
            tt(by_slot, by_slot, nxt.unsqueeze(2).to_broadcast([P, BLOCKS, CHUNK]), ALU.is_lt)
            settle()
            tt(tail_cap[:, :, :], tail_cap[:, :, :], by_slot, ALU.mult)
            settle()
            ts(tail_cap[:, :, :], tail_cap[:, :, :], 0.5, 2.0, ALU.subtract, ALU.mult)
            settle()
            ts(tail_cap[:, :, :], tail_cap[:, :, :], BIG, None, ALU.mult)
            settle()

            def window_of(s):
                return dve.value_load(wide_base[0:1, bass.ds(s.i, 1)], min_val=0, max_val=NP - WIDE)

            def selection(s, ready):
                for half in range(2):
                    sel = ts(select[s.par][:, half, :], iota_f[:, :], place[:, bass.ds(s.i * 2 + half, 1)], None,
                             ALU.is_equal)
                sel.then_inc(ready, 1)

            def weighted_matrix(s):
                dve.wait_ge(edge_in[s.par], s.uses * 48 + 48)
                wait(dve, msg_ps, (s.i - 1) * GROUPS)
                tt(dloc[:, :].rearrange("p (g c) -> p g c", c=COLS),
                   dst_t[s.par][:, :].rearrange("p (g c) -> p g c", c=COLS),
                   base_f[:, bass.ds(s.i * GROUPS, GROUPS)].unsqueeze(2).to_broadcast([P, GROUPS, COLS]),
                   ALU.subtract)
                settle()
                tt(onehot[s.par][:, :, :], dloc[:, :].unsqueeze(2).to_broadcast([P, TILES, WIN]),
                   iota_f[:, 0:WIN].unsqueeze(1).to_broadcast([P, TILES, WIN]), ALU.is_equal)
                settle()
                tt(onehot[s.par][:, :, :], onehot[s.par][:, :, :],
                   w_t[s.par][:, :].unsqueeze(2).to_broadcast([P, TILES, WIN]),
                   ALU.mult).then_inc(wonehot_ready, 1)
                settle()

            def add_sums(s):
                to = out1T[:, bass.ds(window_of(s), WIDE)]
                dve.wait_ge(sumsT_ps, s.i + 1)
                tt(to, to, seg[1][0:EF, 0:WIDE], ALU.add).then_inc(seg_added, 1)
                settle()

            def add_messages(s):
                to = aggT[:, :, bass.ds(window_of(s), WIDE)]
                dve.wait_ge(msgT_ps, s.i + 1)
                tt(to, to, wide[:, 0:KC * WIDE].rearrange("p (c n) -> p c n", c=KC), ALU.add).then_inc(msg_added, 1)
                settle()

            def maxima(s):
                dve.wait_ge(ell_in[s.par], s.uses * 16 * (FULL + 1) + 16 * (FULL + 1))
                tail = ell[s.par][:, FULL * CHUNK * EF:].rearrange("p (k f) -> p k f", f=EF)
                tt(tail, tail, tail_cap[:, bass.ds(s.i, 1), :].rearrange("p a k -> p (a k)")
                   .unsqueeze(2).to_broadcast([P, CHUNK, EF]), ALU.min)
                settle()
                red(chunk_max[:, :, :], ell[s.par].rearrange("p (j k f) -> p j f k", k=CHUNK, f=EF),
                    AX.X, ALU.max).then_inc(ell_used, 1)
                settle()
                tt(chunk_max[:, 0:FULL, :], chunk_max[:, 0:FULL, :],
                   full_cap[:, bass.ds(s.i, 1), :].rearrange("p a j -> p (a j)")
                   .unsqueeze(2).to_broadcast([P, FULL, EF]), ALU.min)
                settle()
                red(max_w[:, :], chunk_max[:, :, :].rearrange("p j f -> p f j"), AX.X, ALU.max)
                settle()
                wait(dve, maxT_ps, s.i - 1)
                ts(max_n[s.par][:, :], max_w[:, :], has[:, bass.ds(s.i, 1)], None, ALU.mult).then_inc(max_ready, 1)

            def mean(m, fast):
                dve.wait_ge(o1_ready, m.i + 1)
                wait(dve, hid_ps, m.i * 2)
                if fast:
                    dve.wait_ge(rinv_in[m.par], m.uses * 16 + 16)
                    by = rinv_b[m.par][:, :]
                else:
                    by = cntT[:, bass.ds(m.i * P, P)]
                tt(o3b[:, :], o1b[:, :], by, ALU.mult).then_inc(mean_ready, 1)

            def moments(v, ready):
                settle()
                dve.bn_stats(stats[:, :], v)
                settle()
                dve.bn_aggr(mv[:, :], stats[:, :]).then_inc(ready, 1)

            def normed(out, v, ready, count):
                dve.wait_ge(ready, count)
                dve.reciprocal(rstd[:, :], std[:, :])
                settle()
                return ts(out, v, mv[:, 0:1], rstd[:, 0:1], ALU.subtract, ALU.mult)

            def norm0(m):
                dve.wait_ge(x_in[m.par], m.uses * 32 + 32)
                dve.scalar_tensor_tensor(out=x2b[:, :], in0=xn_b[m.par][:, :], scalar=2.0, in1=b2_0[:, :],
                                         op0=ALU.mult, op1=ALU.add)
                settle()
                dve.wait_ge(z_ps, m.i + 1)
                tt(z1[:, 0:D], zb[:, 0:D], x2b[:, :], ALU.add)
                moments(z1[:, 0:D], var_ready)
                wait(dve, x1_out[m.par], m.uses * 16)
                normed(out_b[m.par][:, :], z1[:, 0:D], std_ready, m.i + 1).then_inc(x1_ready, 1)

            def aggregate(m):
                dve.wait_ge(x1T_ps, m.i + 1)
                wait(dve, h1_ps, m.i)
                dve.scalar_tensor_tensor(out=agg_in[:, :, :], in0=misc[:, 0:D].rearrange("p (c n) -> p c n", c=KC),
                                         scalar=epsilon[:, 0:1], in1=aggT[:, :, bass.ds(m.i * P, P)],
                                         op0=ALU.mult, op1=ALU.add).then_inc(agg_ready, 1)

            def norm_hidden(m):
                dve.wait_ge(h1_ps, m.i + 1)
                wait(dve, h1T_ps, m.i)
                tt(z1[:, :], hid[0][:, :], b1_1, ALU.add)
                moments(z1[:, :], h1_var)
                normed(z1[:, :], z1[:, :], h1_std, m.i + 1)
                settle()
                tt(z1[:, :], z1[:, :], g1_1, ALU.mult)
                settle()
                tt(z1[:, :], z1[:, :], be1_1, ALU.add).then_inc(h1_ready, 1)

            def norm_out(m):
                y = x2b[:, :]
                dve.wait_ge(h2_ps, m.i + 1)
                tt(y, zb[:, 0:D], b2_1, ALU.add)
                moments(y, out_var)
                normed(y, y, out_std, m.i + 1)
                settle()
                tt(y, y, g2_1, ALU.mult)
                settle()
                tt(y, y, be2_1, ALU.add)
                settle()
                dve.wait_ge(x1_in[m.par], m.uses * 16 + 16)
                dve.scalar_tensor_tensor(out=y, in0=y, scalar=0.0, in1=xn_b[m.par][:, :],
                                         op0=ALU.max, op1=ALU.add)
                moments(y, y_var)
                wait(dve, y_out[m.par], m.uses * 16)
                normed(out_b[m.par][:, :], y, y_std, m.i + 1).then_inc(y_ready, 1)

            def norm1(m):
                aggregate(m)
                norm_hidden(m)
                norm_out(m)

            def last2(m, n):
                for b in (m, n):
                    aggregate(b)
                    norm_hidden(b)
                for b in (m, n):
                    norm_out(b)

            def phase1(s, m):
                early = isinstance(s.i, int) and s.i < 4
                if m is not None and not early:
                    mean(m, True)
                if early:
                    add_sums(s)
                    selection(s.next(), select_ready)
                    if s.i == 1 or s.i == 2:
                        mean(s.before(), True)
                maxima(s)
                if not early:
                    add_sums(s)
                    if not s.last():
                        selection(s.next(), select_ready)
                if m is not None:
                    norm0(m)

            def clear_sums(c):
                dve.memset(aggT[:, c, :], 0.0)
                settle()

            def last1(m):
                mean(m, True)
                clear_sums(m.i - (BLOCKS - 2))
                norm0(m)

            def phase2(s, m):
                selection(s, select1_ready)
                if m is not None:
                    aggregate(m)
                    norm_hidden(m)
                    norm_out(m)
                if not s.last():
                    weighted_matrix(s.next())
                add_messages(s)

            def edge_by_edge(k, from_ps, to, add):
                dve.wait_ge(g_dst_in, k * 16 + 16)
                dve.tensor_copy(to, from_ps)
                settle()
                with dve.Fori(0, P) as e:
                    node = dve.value_load(g_dst[0:1, bass.ds(e, 1)], min_val=0, max_val=NP - 1)
                    add(node, e)
                    settle()
                dve.memset(rstd[:, :], 0.0).then_inc(g_done, 1)
                settle()

            def sum_and_max(node, e):
                row = g_attrT[:, bass.ds(e, 1)]
                tt(out1T[:, bass.ds(node, 1)], out1T[:, bass.ds(node, 1)], row, ALU.add)
                tt(out2T[:, bass.ds(node, 1)], out2T[:, bass.ds(node, 1)], row, ALU.max)
                tt(cntT[:, bass.ds(node, 1)], cntT[:, bass.ds(node, 1)], g_one, ALU.add)

            def add_message(node, e):
                to = aggT[:, :, bass.ds(node, 1)]
                tt(to, to, g_xT[:, :, bass.ds(e, 1)], ALU.add)

            with dve.If(is_fast(dve)):
                selection(at(0), select_ready)
                dve.memset(out1T[:, :], 0.0)
                settle()
                pipelined(dve, phase1, each(last1))
                weighted_matrix(at(0))
                dve.wait_ge(w1_in, 16 * 8)
                pipelined(dve, phase2, last2)
            with dve.Else():
                for half in range(2):
                    dve.wait_ge(attr_in[half], 16)
                dve.memset(out1T[:, :], 0.0)
                dve.memset(out2T, -BIG)
                dve.memset(cntT, 0.0)
                dve.memset(g_one, 1.0)
                settle()
                with dve.Fori(0, GT) as k:
                    dve.wait_ge(g_turned, k + 1)
                    edge_by_edge(k, misc[0:EF, 0:P], g_attrT, sum_and_max)
                ts(g_one, g_one, 1.0, None, ALU.mult)
                settle()
                dve.scalar_tensor_tensor(out=out2T, in0=cntT, scalar=1.0, in1=out2T, op0=ALU.min, op1=ALU.mult)
                settle()
                ts(cntT, cntT, 1.0, None, ALU.max)
                settle()
                dve.reciprocal(cntT, cntT).then_inc(g_sums, 1)
                settle()

                def one(m):
                    mean(m, False)
                    norm0(m)

                over_blocks(dve, one)
                for c in range(KC):
                    clear_sums(c)
                with dve.Fori(0, GT) as k:
                    dve.wait_ge(g_gath_in, k * 16 + 16)
                    dve.wait_ge(g_w_in, k * 16 + 16)
                    ts(g_x, g_x, g_w[:, 0:1], None, ALU.mult).then_inc(g_scaled, 1)
                    dve.wait_ge(g_turned, k + GT + 1)
                    edge_by_edge(k + GT, misc[:, 0:D].rearrange("p (c n) -> p c n", c=KC), g_xT, add_message)
                dve.wait_ge(w1_in, 16 * 8)
                over_blocks(dve, norm1)


def kernel(**a):
    from concourse import bacc
    from concourse.bass_utils import run_bass_kernel_spmd

    pad_e, pad_n = EP - N_EDGES, NP - N_NODES
    a = {k: np.asarray(v) for k, v in a.items()}
    pad_dst = np.repeat(np.arange(N_NODES, NP, dtype=np.int32), PAD_DEG)
    src = np.concatenate([a["src"], np.zeros(pad_e, np.int32)])
    dst = np.concatenate([a["dst"], pad_dst])
    weight = np.concatenate([a["edge_weight"], np.zeros(pad_e, np.float32)])
    attr = np.concatenate([a["edge_attr_96"], np.zeros((pad_e, EF), np.float32)])
    x = np.concatenate([a["x"], np.zeros((pad_n, D), np.float32)])

    def by_step(v):
        return v.reshape(STEPS, GROUPS, P, COLS).transpose(0, 2, 1, 3).reshape(STEPS, P, TILES)

    past = np.concatenate([dst, np.full(1, NP, np.int32)])
    arrays = {
        "attr": attr, "x": x, "xT": x.T,
        "src_s": by_step(src), "dst_s": by_step(dst), "w_s": by_step(weight),
        "src_f": src.reshape(EP, 1), "w_f": weight.reshape(EP, 1), "dst_f": dst.reshape(EP // P, P),
        "keys": dst[::SPLIT], "dst_split": dst.reshape(SPLIT, SPLIT), "base": dst[::GROUP], "ends": dst[GROUP - 1::GROUP],
        "place": np.repeat(dst[::GROUP].reshape(STEPS * 2, GROUPS // 2).T, WIN, axis=0),
        "lane": np.tile(np.arange(WIN, dtype=np.float32), P // WIN).reshape(P, 1),
        "dst_rows": np.concatenate([dst.reshape(ROWS_CHECK, COLS_CHECK),
                                    past[COLS_CHECK::COLS_CHECK].reshape(ROWS_CHECK, 1)], axis=1),
        "W1": a["L0_gnn_W1"], "W2": a["L0_gnn_W2"], "b1_0": a["L0_gnn_b1"].reshape(HC0, P).T,
        "b2_0": a["L0_gnn_b2"], "u0": a["L0_gnn_u"][0].reshape(GF, 1), "epsilon": a["L1_gnn_epsilon"],
        "w1T": a["L1_gnn_w1"].T, "w2T": a["L1_gnn_w2"].T,
        "b1_1": a["L1_gnn_b1"], "g1_1": a["L1_gnn_g1"], "be1_1": a["L1_gnn_beta1"],
        "b2_1": a["L1_gnn_b2"], "g2_1": a["L1_gnn_g2"], "be2_1": a["L1_gnn_beta2"],
    }
    arrays = {k + "_in": np.ascontiguousarray(v) for k, v in arrays.items()}
    nc = bacc.Bacc("TRN2", target_bir_lowering=False, num_devices=1)
    t = {k[:-3]: nc.dram_tensor(k, v.shape, mybir.dt.from_np(v.dtype), kind="ExternalInput").ap()
         for k, v in arrays.items()}
    t["y"] = nc.dram_tensor("y_out_d", (NP, D), F32, kind="ExternalOutput").ap()
    build(nc, t)
    r = run_bass_kernel_spmd(nc, [arrays], core_ids=[0])
    return r.results[0]["y_out_d"][:N_NODES]
```
